# Optimizing a Trainium2 kernel written in Bass

```python
import numpy as np
import jax
import jax.numpy as jnp

def _softmax(x, axis=-1):
    return jax.nn.softmax(x, axis=axis)

def _gelu(x):
    return jax.nn.gelu(x, approximate=True)

def _silu(x):
    return jax.nn.silu(x)

def _sigmoid(x):
    return jax.nn.sigmoid(x)

def _layernorm(x, axis=-1, eps=1e-05):
    m = jnp.mean(x, axis=axis, keepdims=True)
    v = jnp.var(x, axis=axis, keepdims=True)
    return (x - m) / jnp.sqrt(v + eps)

def _scatter_add(tgt, idx, src, axis=0):
    return tgt.at[idx].add(src)

def _segment_sum(src, seg, n):
    return jax.ops.segment_sum(src, seg, n)
kernel_name = 'mk_early_fusion_d1_tok_img768_r4_e32d27'

def setup_inputs(seed: int=0):
    np.random.seed(seed)
    _w = jnp.asarray

    def _rec_inputs():
        import jax
        import jax.numpy as jnp
        _rk = jax.random.key(seed)
        x = -0.00016672 + 0.999947 * jax.random.normal(jax.random.fold_in(_rk, 1), (16, 3, 96, 96), jnp.float32)
        txt = -0.00020034 + 0.55463 * jax.random.normal(jax.random.fold_in(_rk, 2), (16, 32, 192), jnp.float32)
        return (x, txt)
    x, txt = _rec_inputs()

    def _L0_tok_setup():
        import jax, jax.numpy as jnp
        import numpy as np
        B, C, H, W_IMG = (64, 3, 96, 96)
        P = 16
        E = 192
        key = jax.random.key(seed)
        k1, k2, k3 = jax.random.split(key, 3)
        x = jax.random.normal(k1, (B, C, H, W_IMG), dtype=jnp.float32)
        W = jax.random.normal(k2, (E, C * P * P), dtype=jnp.float32) * 0.02
        bias = jax.random.normal(k3, (E,), dtype=jnp.float32) * 0.02
        return {'x': x, 'W': W, 'bias': bias}
    _L0_tok_all = _L0_tok_setup()
    _L0_tok_in = {k: v for k, v in _L0_tok_all.items() if k in ('W', 'bias')}
    del _L0_tok_all

    def _L0_attn_setup():
        import jax, jax.numpy as jnp
        import numpy as np
        NUM_HEADS = 12
        SCRA_SCALING = 10.0
        EPS = 1e-12
        key = jax.random.key(seed)
        ks = jax.random.split(key, 5)
        B, N, C = (2, 512, 192)
        return {'x': jax.random.normal(ks[0], (B, N, C), dtype=jnp.float32), 'qkv_w': jax.random.normal(ks[1], (3 * C, C), dtype=jnp.float32) * 0.02, 'qkv_b': jax.random.normal(ks[2], (3 * C,), dtype=jnp.float32) * 0.02, 'proj_w': jax.random.normal(ks[3], (C, C), dtype=jnp.float32) * 0.02, 'proj_b': jax.random.normal(ks[4], (C,), dtype=jnp.float32) * 0.02}
    _L0_attn_all = _L0_attn_setup()
    _L0_attn_in = {k: v for k, v in _L0_attn_all.items() if k in ('qkv_w', 'qkv_b', 'proj_w', 'proj_b')}
    del _L0_attn_all

    def _L0_ffn_setup():
        import jax, jax.numpy as jnp
        import numpy as np
        D = 192
        M = 768
        G = 4
        E = 8
        KG = 2
        KE = 4
        EPS = 1e-06

        def _topk_gates(logits, k):
            top, idx = jax.lax.top_k(logits, k)
            gates = jax.nn.softmax(top, axis=-1)
            gates = jnp.where(gates >= EPS, gates, jnp.zeros_like(gates))
            return (gates, idx)
        key = jax.random.key(seed)
        ks = jax.random.split(key, 9)
        x = jax.random.normal(ks[0], (1, 256, D), dtype=jnp.float32)
        Wg = jax.random.normal(ks[1], (D, G), dtype=jnp.float32) * 0.02
        bg = jax.random.normal(ks[2], (G,), dtype=jnp.float32) * 0.01
        We = jax.random.normal(ks[3], (G, D, E), dtype=jnp.float32) * 0.02
        be = jax.random.normal(ks[4], (G, E), dtype=jnp.float32) * 0.01
        W1 = jax.random.normal(ks[5], (G, E, D, M), dtype=jnp.float32) * 0.02
        b1 = jax.random.normal(ks[6], (G, E, M), dtype=jnp.float32) * 0.01
        W2 = jax.random.normal(ks[7], (G, E, M, D), dtype=jnp.float32) * 0.02
        b2 = jax.random.normal(ks[8], (G, E, D), dtype=jnp.float32) * 0.01
        return {'x': x, 'Wg': Wg, 'bg': bg, 'We': We, 'be': be, 'W1': W1, 'b1': b1, 'W2': W2, 'b2': b2}
    _L0_ffn_all = _L0_ffn_setup()
    _L0_ffn_in = {k: v for k, v in _L0_ffn_all.items() if k in ('Wg', 'bg', 'We', 'be', 'W1', 'b1', 'W2', 'b2')}
    del _L0_ffn_all
    return {'x': x, 'txt': txt, 'L0_tok_W': _L0_tok_in['W'], 'L0_tok_bias': _L0_tok_in['bias'], 'L0_attn_qkv_w': _L0_attn_in['qkv_w'], 'L0_attn_qkv_b': _L0_attn_in['qkv_b'], 'L0_attn_proj_w': _L0_attn_in['proj_w'], 'L0_attn_proj_b': _L0_attn_in['proj_b'], 'L0_ffn_Wg': _L0_ffn_in['Wg'], 'L0_ffn_bg': _L0_ffn_in['bg'], 'L0_ffn_We': _L0_ffn_in['We'], 'L0_ffn_be': _L0_ffn_in['be'], 'L0_ffn_W1': _L0_ffn_in['W1'], 'L0_ffn_b1': _L0_ffn_in['b1'], 'L0_ffn_W2': _L0_ffn_in['W2'], 'L0_ffn_b2': _L0_ffn_in['b2']}

def reference(x, txt, L0_tok_W, L0_tok_bias, L0_attn_qkv_w, L0_attn_qkv_b, L0_attn_proj_w, L0_attn_proj_b, L0_ffn_Wg, L0_ffn_bg, L0_ffn_We, L0_ffn_be, L0_ffn_W1, L0_ffn_b1, L0_ffn_W2, L0_ffn_b2):
    import jax
    import jax.numpy as jnp

    def _L0_tok_ref(x, W, bias):
        import jax, jax.numpy as jnp
        import numpy as np
        B, C, H, W_IMG = (64, 3, 96, 96)
        P = 16
        E = 192
        b, c, h, w = x.shape
        ph, pw = (h // P, w // P)
        patches = x.reshape(b, c, ph, P, pw, P)
        patches = patches.transpose(0, 2, 4, 1, 3, 5).reshape(b, ph * pw, c * P * P)
        return jnp.einsum('bnd,ed->bne', patches, W) + bias

    def _L0_attn_ref(x, qkv_w, qkv_b, proj_w, proj_b):
        import jax, jax.numpy as jnp
        import numpy as np
        NUM_HEADS = 12
        SCRA_SCALING = 10.0
        EPS = 1e-12
        B, N, C = x.shape
        H = NUM_HEADS
        D = C // H
        scale = D ** (-0.5)
        xt = jnp.transpose(x, (1, 0, 2))
        qkv = xt @ qkv_w.T + qkv_b
        q, k, v = jnp.split(qkv, 3, axis=-1)

        def to_bh(t):
            return jnp.transpose(t.reshape(N, B * H, D), (1, 0, 2))
        q, k, v = (to_bh(q), to_bh(k), to_bh(v))
        attn = jax.nn.softmax(jnp.einsum('bnd,bmd->bnm', q, k) * scale, axis=-1)
        out = jnp.einsum('bnm,bmd->bnd', attn, v)
        out = jnp.transpose(out, (1, 0, 2)).reshape(N, B, C)
        out = out @ proj_w.T + proj_b
        out = jnp.transpose(out.reshape(N, B * H, D), (1, 0, 2))
        norm = jnp.linalg.norm(out, axis=-1, keepdims=True)
        sim_tokens = out / jnp.maximum(norm, EPS)
        sim = jnp.einsum('bnd,bmd->bnm', sim_tokens, sim_tokens) * SCRA_SCALING
        sim = jnp.where(sim < 0, -jnp.inf, sim)
        sim = jax.nn.softmax(sim, axis=-1)
        out2 = jnp.einsum('bnm,bmd->bnd', sim, v)
        out2 = jnp.transpose(out2, (1, 0, 2)).reshape(N, B, C)
        out2 = out2 @ proj_w.T + proj_b
        return jnp.transpose(out2, (1, 0, 2))

    def _L0_ffn_ref(x, Wg, bg, We, be, W1, b1, W2, b2):
        import jax, jax.numpy as jnp
        import numpy as np
        D = 192
        M = 768
        G = 4
        E = 8
        KG = 2
        KE = 4
        EPS = 1e-06

        def _topk_gates(logits, k):
            top, idx = jax.lax.top_k(logits, k)
            gates = jax.nn.softmax(top, axis=-1)
            gates = jnp.where(gates >= EPS, gates, jnp.zeros_like(gates))
            return (gates, idx)
        orig_shape = x.shape
        xf = x.reshape(-1, D)
        glog = xf @ Wg + bg
        ggates, gidx = _topk_gates(glog, KG)
        gw = jnp.einsum('nk,nkg->ng', ggates, jax.nn.one_hot(gidx, G, dtype=xf.dtype))
        elog = jnp.einsum('nd,gde->nge', xf, We) + be
        egates, eidx = _topk_gates(elog, KE)
        ew = jnp.einsum('ngk,ngke->nge', egates, jax.nn.one_hot(eidx, E, dtype=xf.dtype))
        combine = gw[:, :, None] * ew
        y = jnp.zeros_like(xf)
        for g in range(G):
            h = jax.nn.gelu(jnp.einsum('nd,edm->enm', xf, W1[g]) + b1[g][:, None, :], approximate=False)
            o = jnp.einsum('enm,emd->end', h, W2[g]) + b2[g][:, None, :]
            y = y + jnp.einsum('end,ne->nd', o, combine[:, g, :])
        return y.reshape(orig_shape)
    h = _L0_tok_ref(x, L0_tok_W, L0_tok_bias)
    h = jnp.concatenate([h, txt], axis=1)
    h = h + _L0_attn_ref(_layernorm(h, axis=-1), L0_attn_qkv_w, L0_attn_qkv_b, L0_attn_proj_w, L0_attn_proj_b)
    h = h + _L0_ffn_ref(_layernorm(h, axis=-1), L0_ffn_Wg, L0_ffn_bg, L0_ffn_We, L0_ffn_be, L0_ffn_W1, L0_ffn_b1, L0_ffn_W2, L0_ffn_b2)
    return h

_drawn_inputs = setup_inputs


def setup_inputs(seed=0):
    import zlib

    import numpy as np

    out = dict(_drawn_inputs(seed))
    spreads = {}
    factors = {'L0_attn_qkv_w': 3.215,
     'L0_attn_qkv_b': 5.274,
     'L0_ffn_bg': 6.573,
     'L0_ffn_be': 8.0,
     'L0_ffn_b1': 28.66,
     'L0_ffn_b2': 8.0}
    for name, (base, spread) in spreads.items():
        noise = np.random.default_rng([zlib.crc32(name.encode()), seed]).standard_normal(out[name].shape)
        drawn = base * np.exp(spread * noise) if base else spread * noise
        out[name] = jnp.asarray(drawn.astype(out[name].dtype))
    for name, factor in factors.items():
        out[name] = (out[name] * factor).astype(out[name].dtype)
    return out
```

```python
from contextlib import ExitStack

import concourse.bass as bass
from concourse import mybir

F32 = mybir.dt.float32
ALU = mybir.AluOpType
ACT = mybir.ActivationFunctionType
AX = mybir.AxisListType

B = 16
PATCH_TOK = 36
T = 68
D = 192
HALF = 96
HEADS, HD = 12, 16
HG = HEADS // 2
PIX = 768
PK = PIX // 128
G, E = 4, 8
NE = G * E
KG, KE = 2, 4
HID = 768
HC = HID // 128
R = G + NE
LN_EPS = 1e-5
GATE_EPS = 1e-6
NORM_EPS = 1e-12
ATT_SCALE = HD ** -0.5
SIM_SCALE = 10.0


def build(nc, patches, tok_w, tok_b, txt, qkv_w, proj_w, router_w, w1, b1, w2, b2,
          identity, head_mask, earlier, out):
    with ExitStack() as ctx:
        def sb(name, shape):
            return ctx.enter_context(nc.sbuf_tensor(name, shape, F32))

        def sem(name):
            return ctx.enter_context(nc.semaphore(name))

        patches_sb = sb("patches_sb", [128, PK, PATCH_TOK])
        tok_w_sb = sb("tok_w_sb", [128, PK, D])
        tok_b_sb = sb("tok_b_sb", [PATCH_TOK, D])
        qkv_w_sb = sb("qkv_w_sb", [HALF + 1, 2, 3 * D])
        proj_w_sb = sb("proj_w_sb", [HALF + 1, 2, D])
        router_w_sb = sb("router_w_sb", [HALF + 1, 2, R])
        ident = sb("ident", [T, T])
        head_mask_sb = sb("head_mask_sb", [HALF, HG])
        earlier_sb = sb("earlier_sb", [T, E, E])
        eps = sb("eps", [T, 1])
        minus_half = sb("minus_half", [T, HEADS])
        b2_sb = sb("b2_sb", [NE, D])

        h_sb = sb("h_sb", [T, B, D])
        v_sb = sb("v_sb", [T, B, HEADS, HD + 1])
        xf_T = sb("xf_T", [HALF + 1, 2, B, T])
        logits = sb("logits", [T, B, R])

        stats = sb("stats", [T, 6])
        mean_var = sb("mean_var", [T, 2])
        var_eps = sb("var_eps", [T, 1])
        rstd = sb("rstd", [T, 1])
        stats2 = sb("stats2", [T, 6])
        mean_var2 = sb("mean_var2", [T, 2])
        var_eps2 = sb("var_eps2", [T, 1])
        rstd2 = sb("rstd2", [T, 1])
        xn = sb("xn", [T, D])
        xn_T = sb("xn_T", [HALF + 1, 2, T])
        qk_T = sb("qk_T", [HALF, 4, T])
        k_wide = sb("k_wide", [HALF, 2, HG, T])
        row_max = sb("row_max", [T, HEADS])
        shifted = sb("shifted", [T, HEADS, T])
        probs_T = sb("probs_T", [T, HEADS, T])
        sum_inv = sb("sum_inv", [T, HEADS])
        o1 = sb("o1", [T, D])
        o1_T = sb("o1_T", [HALF + 1, 2, T])
        squares = sb("squares", [T, HEADS, HD])
        norm2 = sb("norm2", [T, HEADS])
        norm2_clamped = sb("norm2_clamped", [T, HEADS])
        norm_inv = sb("norm_inv", [T, HEADS])
        t_tok = sb("t_tok", [T, D])
        t_T = sb("t_T", [HALF, 2, T])
        t_wide = sb("t_wide", [HALF, 2, HG, T])
        sim_exp = sb("sim_exp", [T, HEADS, T])
        sim_probs = sb("sim_probs", [T, HEADS, T])
        sum2_inv = sb("sum2_inv", [T, HEADS])
        o2 = sb("o2", [T, D])
        o2_T = sb("o2_T", [HALF + 1, 2, T])
        xf = sb("xf", [T, D])
        xf_cur = sb("xf_cur", [HALF + 1, 2, T])

        beats = sb("beats", [T, B * G, E, E])
        ties = sb("ties", [T, B * G, E, E])
        e_rank = sb("e_rank", [T, B * G, E])
        e_max = sb("e_max", [T, B * G])
        e_exp = sb("e_exp", [T, B * G, E])
        e_gate = sb("e_gate", [T, B * G, E])
        e_sum = sb("e_sum", [T, B * G])
        e_inv = sb("e_inv", [T, B * G])
        g_rank = sb("g_rank", [T, B, G])
        g_max = sb("g_max", [T, B])
        g_exp = sb("g_exp", [T, B, G])
        g_gate = sb("g_gate", [T, B, G])
        g_sum = sb("g_sum", [T, B])
        g_inv = sb("g_inv", [T, B])
        combine = sb("combine", [T, B, NE])
        combine_T = sb("combine_T", [NE, T])
        ex_logits = sb("ex_logits", [T, B * G, E])
        w1_sb = [sb(f"w1_sb{i}", [HALF, 2, HID]) for i in range(2)]
        w2_sb = [sb(f"w2_sb{i}", [128, HC, D]) for i in range(2)]
        b1_sb = [sb(f"b1_sb{i}", [128, HC]) for i in range(2)]
        hid = sb("hid", [128, HC, 4 * T])
        w1_in = [sem(f"w1_in{i}") for i in range(2)]
        w2_in = [sem(f"w2_in{i}") for i in range(2)]

        bank = [ctx.enter_context(nc.psum_tensor(f"bank{i}", [128, 512], F32)) for i in range(8)]

        names = """stored patches_in xf_kept loaded consts_set mask2_done exp2_done turned scores_exped pv2_done tok_done h_read
        stats_done meanvar_done vareps_done rstd_done xn_done xnT_done xnT_copied o2_recip o2_done o2T_done
        o2T_copied pv_done o1_recip o1_done qk_done v_done proj2_done o1T_done qk_copied v_copied
        o1T_copied h2_done stats2_done meanvar2_done vareps2_done rstd2_done k_wide_done proj1_done
        squared xf_done norm2_done scores_done xfT_done normclamp_done norminv_done t_done tT_done
        xfT_copied tT_copied router_done logits_copied t_wide_done max_done shifted_done sim_done
        d e_ready e_exped g_ready g_exped combine_done cT_done cT_copied b2_done y0_done g1_done hid_done g2_done y_done""".split()
        S = {n: sem(n) for n in names}

        loads = [
            (tok_w_sb, tok_w), (tok_b_sb, tok_b), (qkv_w_sb, qkv_w),
            (proj_w_sb, proj_w), (router_w_sb, router_w), (ident, identity),
            (head_mask_sb, head_mask), (earlier_sb, earlier), (b2_sb, b2),
        ]
        loads_done = 16 * (len(loads) + 1)

        def wait(eng, name, b):
            if isinstance(b, int) and b < 0:
                return
            eng.wait_ge(S[name], b + 1)

        def apart(eng):
            eng.wait_ge(S["consts_set"], 8)

        def pipeline(eng, body):
            for i in range(3):
                body(i)
            with eng.Fori(3, B) as i:
                body(i)
            for i in range(B, B + 2):
                body(i)

        def stages(i):
            if not isinstance(i, int):
                return i, i - 1, i - 2
            return (i if i < B else None), (i - 1 if 1 <= i <= B else None), (i - 2 if i >= 2 else None)

        scores_bank = [bank[0], bank[1]]
        sim_bank = [bank[2], bank[3]]
        block = ctx.enter_context(nc.Block())

        @block.sync
        def _(sp):
            for dst, src in loads:
                sp.dma_start(dst[:], src).then_inc(S["loaded"], 16)
            sp.dma_start(h_sb[PATCH_TOK:T, :, :], txt).then_inc(S["loaded"], 16)

            def patches_of(a):
                wait(sp, "tok_done", a - 1)
                sp.dma_start(patches_sb[:], patches[a]).then_inc(S["patches_in"], 16)
            patches_of(0)
            with sp.Fori(1, B) as a:
                patches_of(a)

            def load(e, p, first):
                if not first:
                    sp.wait_ge(S["g2_done"], 16 * (e - 1))
                sp.dma_start(b1_sb[p][:], b1[e]).then_inc(w1_in[p], 16)
                sp.dma_start(w1_sb[p][:], w1[e]).then_inc(w1_in[p], 16)
                sp.dma_start(w2_sb[p][:], w2[e]).then_inc(w2_in[p], 16)
            load(0, 0, True)
            load(1, 1, True)
            with sp.Fori(1, NE // 2) as q:
                load(2 * q, 0, False)
                load(2 * q + 1, 1, False)
            sp.wait_ge(S["y_done"], 16 * NE)
            sp.dma_start(out, h_sb[:]).then_inc(S["stored"], 16)
            sp.wait_ge(S["stored"], 16)

        @block.gpsimd
        def _(pool):
            pool.memset(minus_half[:], -0.5).then_inc(S["consts_set"], 1)
            pool.memset(eps[:], LN_EPS).then_inc(S["consts_set"], 1)
            for buf in (xn_T, o1_T, o2_T, xf_cur):
                pool.memset(buf[HALF:HALF + 1, :, :], 1.0).then_inc(S["consts_set"], 1)
            pool.memset(xf_T[HALF:HALF + 1, :, :, :], 1.0).then_inc(S["consts_set"], 1)
            pool.memset(v_sb[:, :, :, HD:HD + 1], 1.0).then_inc(S["consts_set"], 1)
            pool.wait_ge(S["consts_set"], 8)
            pool.wait_ge(S["loaded"], loads_done)

            def inverse_root(mv, tmp, dst, done1, done2, b):
                pool.tensor_tensor(tmp[:], mv[:, 1:2], eps[:], ALU.add).then_inc(S[done1], 1)
                wait(pool, done1, b)
                pool.tensor_tensor(dst[:], tmp[:], minus_half[:, 0:1], ALU.pow).then_inc(S[done2], 1)

            def widen(dst, src, done):
                for g in range(2):
                    ins = pool.tensor_tensor(
                        dst[:, g, :, :], src(g).unsqueeze(1).to_broadcast([HALF, HG, T]),
                        head_mask_sb[:, :].unsqueeze(2).to_broadcast([HALF, HG, T]), ALU.mult)
                ins.then_inc(S[done], 1)

            def turn(i):
                a, b, c = stages(i)
                if a is not None:
                    wait(pool, "meanvar_done", a)
                    inverse_root(mean_var, var_eps, rstd, "vareps_done", "rstd_done", a)
                if c is not None:
                    wait(pool, "meanvar2_done", c)
                    inverse_root(mean_var2, var_eps2, rstd2, "vareps2_done", "rstd2_done", c)
                if a is not None:
                    wait(pool, "qk_copied", a)
                    wait(pool, "scores_done", a - 1)
                    widen(k_wide, lambda g: qk_T[:, 2 + g, :], "k_wide_done")
                if b is not None:
                    apart(pool)
                    wait(pool, "norm2_done", b)
                    wait(pool, "t_done", b - 1)
                    pool.tensor_scalar(norm2_clamped[:], norm2[:], NORM_EPS ** 2, None,
                                       ALU.max).then_inc(S["normclamp_done"], 1)
                    wait(pool, "normclamp_done", b)
                    pool.tensor_tensor(norm_inv[:], norm2_clamped[:], minus_half[:],
                                       ALU.pow).then_inc(S["norminv_done"], 1)
                    wait(pool, "tT_copied", b)
                    wait(pool, "sim_done", b - 1)
                    widen(t_wide, lambda g: t_T[:, g, :], "t_wide_done")
                if c is not None:
                    wait(pool, "xfT_copied", c)
                    pool.tensor_copy(xf_T[0:HALF, :, c, :], xf_cur[0:HALF, :, :]).then_inc(S["xf_kept"], 1)

            pipeline(pool, turn)

        @block.scalar
        def _(act):
            act.wait_ge(S["consts_set"], 8)

            def copy_halves(dst, psum, done):
                act.activation(dst, psum[0:HALF, 0:2 * T].rearrange("p (g t) -> p g t", g=2),
                               ACT.Copy).then_inc(S[done], 1)

            def turn(i):
                a, b, c = stages(i)
                if c is not None:
                    wait(act, "sim_done", c)
                    wait(act, "mask2_done", c - 1)
                    for g in range(2):
                        ins = act.activation(sim_exp[:, g * HG:(g + 1) * HG, :].rearrange("p h t -> p (h t)"),
                                             sim_bank[g][0:T, 0:HG * T], ACT.Exp, scale=SIM_SCALE)
                    ins.then_inc(S["exp2_done"], 1)
                if b is not None:
                    wait(act, "turned", b)
                    wait(act, "pv_done", b - 1)
                    for g in range(2):
                        ins = act.activation(probs_T[:, g * HG:(g + 1) * HG, :].rearrange("p h t -> p (h t)"),
                                             scores_bank[g][0:T, 0:HG * T], ACT.Exp, scale=ATT_SCALE)
                    ins.then_inc(S["scores_exped"], 1)
                if a is not None:
                    wait(act, "xnT_done", a)
                    wait(act, "v_done", a - 1)
                    copy_halves(xn_T[0:HALF, :, :], bank[7], "xnT_copied")
                if c is not None:
                    wait(act, "o2T_done", c)
                    wait(act, "proj2_done", c - 1)
                    copy_halves(o2_T[0:HALF, :, :], bank[6], "o2T_copied")
                if a is not None:
                    wait(act, "qk_done", a)
                    wait(act, "k_wide_done", a - 1)
                    wait(act, "scores_done", a - 1)
                    act.activation(qk_T[:].rearrange("p q t -> p (q t)"), bank[6][0:HALF, 0:4 * T],
                                   ACT.Copy).then_inc(S["qk_copied"], 1)
                    apart(act)
                    wait(act, "v_done", a)
                    act.activation(v_sb[:, a, :, 0:HD],
                                   bank[7][0:T, 0:D].rearrange("p (h d) -> p h d", h=HEADS),
                                   ACT.Copy).then_inc(S["v_copied"], 1)
                if b is not None:
                    wait(act, "o1T_done", b)
                    wait(act, "proj1_done", b - 1)
                    copy_halves(o1_T[0:HALF, :, :], bank[4], "o1T_copied")
                    wait(act, "proj1_done", b)
                    wait(act, "norm2_done", b - 1)
                    act.activation(squares[:].rearrange("p h d -> p (h d)"), bank[6][0:T, 0:D],
                                   ACT.Square).then_inc(S["squared"], 1)
                if c is not None:
                    wait(act, "xfT_done", c)
                    wait(act, "router_done", c - 1)
                    wait(act, "xf_kept", c - 1)
                    copy_halves(xf_cur[0:HALF, :, :], bank[5], "xfT_copied")
                if b is not None:
                    wait(act, "tT_done", b)
                    wait(act, "sim_done", b - 1)
                    wait(act, "t_wide_done", b - 1)
                    copy_halves(t_T[:], bank[4], "tT_copied")
                if c is not None:
                    apart(act)
                    wait(act, "router_done", c)
                    act.activation(logits[:, c, :], bank[7][0:T, 0:R], ACT.Copy).then_inc(S["logits_copied"], 1)

            pipeline(act, turn)
            act.wait_ge(S["e_ready"], 1)
            act.activation(e_exp[:], ex_logits[:], ACT.Exp).then_inc(S["e_exped"], 1)
            act.wait_ge(S["g_ready"], 1)
            act.activation(g_exp[:], g_exp[:], ACT.Exp).then_inc(S["g_exped"], 1)
            for b in range(B):
                wait(act, "cT_done", b)
                wait(act, "b2_done", b - 1)
                act.activation(combine_T[:], bank[b % 2][0:NE, 0:T], ACT.Copy).then_inc(S["cT_copied"], 1)

            def expert(e, p, turns):
                act.wait_ge(w1_in[p], 32 * turns)
                for tc in range(4):
                    for c in range(HC):
                        act.wait_ge(S["g1_done"], e * 24 + tc * 6 + c + 1)
                        if c == 0:
                            if not (isinstance(e, int) and e == 0 and tc == 0):
                                act.wait_ge(S["g2_done"], e * 16 + tc * 4)
                        act.activation(hid[:, c, :], bank[c % 3][:, 0:4 * T], ACT.Gelu,
                                       bias=b1_sb[p][:, c:c + 1]).then_inc(S["hid_done"], 1)
            expert(0, 0, 1)
            expert(1, 1, 1)
            with act.Fori(1, NE // 2) as q:
                expert(2 * q, 0, q + 1)
                expert(2 * q + 1, 1, q + 1)

        @block.tensor
        def _(pe):
            pe.wait_ge(S["loaded"], loads_done)
            pe.wait_ge(S["consts_set"], 8)

            def turn_halves(psum, src, done):
                for g in range(2):
                    ins = pe.transpose(psum[0:HALF, g * T:(g + 1) * T], src[:, g * HALF:(g + 1) * HALF], ident[:])
                ins.then_inc(S[done], 1)

            def linear(psum, x_T, w, done):
                for g in range(2):
                    k = HALF + g
                    ins = pe.matmul(psum, x_T[0:k, g], w[0:k, g, :], start=(g == 0), stop=(g == 1))
                ins.then_inc(S[done], 1)

            def weighted_values(psum, weights, b, done):
                for h in range(HEADS):
                    ins = pe.matmul(psum[0:T, h * (HD + 1):(h + 1) * (HD + 1)], weights[:, h, :],
                                    v_sb[:, b, h, :], start=True, stop=True)
                ins.then_inc(S[done], 1)

            def turn(i):
                a, b, c = stages(i)
                if b is not None:
                    wait(pe, "shifted_done", b)
                    for h in range(HEADS):
                        ins = pe.transpose(scores_bank[h // HG][0:T, h % HG * T:(h % HG + 1) * T],
                                           shifted[:, h, :], ident[:])
                    ins.then_inc(S["turned"], 1)
                if c is not None:
                    wait(pe, "mask2_done", c)
                    wait(pe, "tT_copied", c)
                    weighted_values(bank[4], sim_probs, c, "pv2_done")
                if a is not None:
                    wait(pe, "xfT_copied", a - 3)
                    wait(pe, "h_read", a - 1)
                    pe.wait_ge(S["patches_in"], 16 * (a + 1))
                    for k in range(PK):
                        ins = pe.matmul(bank[5][0:PATCH_TOK, 0:D], patches_sb[:, k, :] if isinstance(a, int)
                                        else patches_sb[:, k, :], tok_w_sb[:, k, :],
                                        start=(k == 0), stop=(k == PK - 1))
                    ins.then_inc(S["tok_done"], 1)
                    wait(pe, "xn_done", a)
                    wait(pe, "logits_copied", a - 3)
                    wait(pe, "v_copied", a - 1)
                    turn_halves(bank[7], xn, "xnT_done")
                if c is not None:
                    wait(pe, "o2_done", c)
                    wait(pe, "t_done", c)
                    turn_halves(bank[6], o2, "o2T_done")
                if b is not None:
                    wait(pe, "scores_exped", b)
                    wait(pe, "tT_copied", b - 1)
                    if c is not None:
                        wait(pe, "o2_done", c)
                    weighted_values(bank[4], probs_T, b, "pv_done")
                if a is not None:
                    wait(pe, "xnT_copied", a)
                    if c is not None:
                        wait(pe, "o2T_copied", c)
                    for q in range(4):
                        for g in range(2):
                            k = HALF + g
                            ins = pe.matmul(bank[6][0:HALF, q * T:(q + 1) * T],
                                            qkv_w_sb[0:k, g, q * HALF:(q + 1) * HALF], xn_T[0:k, g, :],
                                            start=(g == 0), stop=(g == 1))
                    ins.then_inc(S["qk_done"], 1)
                    linear(bank[7][0:T, 0:D], xn_T, qkv_w_sb[:, :, 2 * D:3 * D], "v_done")
                if c is not None:
                    wait(pe, "o2T_copied", c)
                    if a is not None:
                        wait(pe, "h_read", a)
                    linear(bank[5][0:T, 0:D], o2_T, proj_w_sb, "proj2_done")
                if b is not None:
                    wait(pe, "o1_done", b)
                    turn_halves(bank[4], o1, "o1T_done")
                    wait(pe, "o1T_copied", b)
                    if a is not None:
                        wait(pe, "qk_copied", a)
                    linear(bank[6][0:T, 0:D], o1_T, proj_w_sb, "proj1_done")
                if a is not None:
                    wait(pe, "k_wide_done", a)
                    if b is not None:
                        wait(pe, "scores_exped", b)
                    for g in range(2):
                        ins = pe.matmul(scores_bank[g][0:T, 0:HG * T], qk_T[:, g, :],
                                        k_wide[:, g, :, :].rearrange("p h t -> p (h t)"), start=True, stop=True)
                    ins.then_inc(S["scores_done"], 1)
                if c is not None:
                    wait(pe, "xf_done", c)
                    turn_halves(bank[5], xf, "xfT_done")
                if b is not None:
                    wait(pe, "t_done", b)
                    turn_halves(bank[4], t_tok, "tT_done")
                if c is not None:
                    wait(pe, "xfT_copied", c)
                    wait(pe, "logits_copied", c - 1)
                    if a is not None:
                        wait(pe, "v_copied", a)
                    linear(bank[7][0:T, 0:R], xf_cur, router_w_sb, "router_done")
                if b is not None:
                    wait(pe, "t_wide_done", b)
                    wait(pe, "mask2_done", b - 1)
                    for g in range(2):
                        ins = pe.matmul(sim_bank[g][0:T, 0:HG * T], t_T[:, g, :],
                                        t_wide[:, g, :, :].rearrange("p h t -> p (h t)"), start=True, stop=True)
                    ins.then_inc(S["sim_done"], 1)

            pipeline(pe, turn)
            pe.wait_ge(S["combine_done"], 1)
            wait(pe, "xf_kept", B - 1)
            for b in range(B):
                wait(pe, "cT_copied", b - 2)
                pe.transpose(bank[b % 2][0:NE, 0:T], combine[:, b, :], ident[:]).then_inc(S["cT_done"], 1)
                wait(pe, "cT_copied", b)
                wait(pe, "y0_done", b - 2)
                pe.matmul(bank[2 + b % 2][0:T, 0:D], combine_T[:], b2_sb[:], start=True,
                          stop=True).then_inc(S["b2_done"], 1)
            wait(pe, "y0_done", B - 1)

            def expert(e, p, turns):
                pe.wait_ge(w1_in[p], 32 * turns)
                pe.wait_ge(w2_in[p], 16 * turns)
                for tc in range(4):
                    for c in range(HC):
                        if not (isinstance(e, int) and e == 0 and tc == 0 and c < 3):
                            pe.wait_ge(S["hid_done"], e * 24 + tc * 6 + c - 2)
                        for g in range(2):
                            ins = pe.matmul(bank[c % 3][:, 0:4 * T], w1_sb[p][:, g, c * 128:(c + 1) * 128],
                                            xf_T[0:HALF, g, 4 * tc:4 * tc + 4, :].rearrange("p b t -> p (b t)"),
                                            start=(g == 0), stop=(g == 1))
                        ins.then_inc(S["g1_done"], 1)
                    pe.wait_ge(S["hid_done"], e * 24 + tc * 6 + 6)
                    for j in range(4):
                        if not (isinstance(e, int) and e == 0 and tc == 0):
                            pe.wait_ge(S["y_done"], e * 16 + tc * 4 + j - 3)
                        for c in range(HC):
                            ins = pe.matmul(bank[4 + j][0:T, 0:D], hid[:, c, j * T:(j + 1) * T], w2_sb[p][:, c, :],
                                            start=(c == 0), stop=(c == HC - 1))
                        ins.then_inc(S["g2_done"], 1)
            expert(0, 0, 1)
            expert(1, 1, 1)
            with pe.Fori(1, NE // 2) as q:
                expert(2 * q, 0, q + 1)
                expert(2 * q + 1, 1, q + 1)

        @block.vector
        def _(dve):
            dve.wait_ge(S["loaded"], loads_done)
            dve.wait_ge(S["consts_set"], 8)

            def by_head(psum):
                return psum[0:T, 0:HEADS * (HD + 1)].rearrange("p (h d) -> p h d", h=HEADS)

            def normalise(psum, inv, dst, free, recip, done, b):
                pv = by_head(psum)
                wait(dve, done, b - 1)
                dve.reciprocal(inv[:].unsqueeze(2), pv[:, :, HD:HD + 1]).then_inc(S[recip], 1)
                wait(dve, recip, b)
                wait(dve, free, b - 1)
                dve.tensor_tensor(dst[:].rearrange("p (h d) -> p h d", h=HEADS), pv[:, :, 0:HD],
                                  inv[:].unsqueeze(2).to_broadcast([T, HEADS, HD]), ALU.mult).then_inc(S[done], 1)

            def moments(src, st, mv, h_ready, st_done, free, done, b):
                apart(dve)
                wait(dve, h_ready, b)
                wait(dve, done, b - 1)
                dve.bn_stats(st[:], src).then_inc(S[st_done], 1)
                apart(dve)
                wait(dve, st_done, b)
                wait(dve, free, b - 1)
                dve.bn_aggr(mv[:], st[:]).then_inc(S[done], 1)

            def turn(i):
                a, b, c = stages(i)
                if c is not None:
                    wait(dve, "exp2_done", c)
                    wait(dve, "pv2_done", c - 1)
                    for g in range(2):
                        ins = dve.scalar_tensor_tensor(
                            sim_probs[:, g * HG:(g + 1) * HG, :].rearrange("p h t -> p (h t)"),
                            sim_bank[g][0:T, 0:HG * T], 0.0,
                            sim_exp[:, g * HG:(g + 1) * HG, :].rearrange("p h t -> p (h t)"), ALU.is_ge, ALU.mult)
                    ins.then_inc(S["mask2_done"], 1)
                if a is not None:
                    wait(dve, "tok_done", a)
                    dve.tensor_tensor(h_sb[0:PATCH_TOK, a, :], bank[5][0:PATCH_TOK, 0:D], tok_b_sb[:],
                                      ALU.add).then_inc(S["h_read"], 1)
                    moments(h_sb[:, a, :], stats, mean_var, "h_read", "stats_done", "xn_done", "meanvar_done", a)
                    wait(dve, "rstd_done", a)
                    wait(dve, "xnT_done", a - 1)
                    dve.tensor_scalar(xn[:], h_sb[:, a, :], mean_var[:, 0:1], rstd[:], ALU.subtract,
                                      ALU.mult).then_inc(S["xn_done"], 1)
                if c is not None:
                    wait(dve, "pv2_done", c)
                    normalise(bank[4], sum2_inv, o2, "o2T_done", "o2_recip", "o2_done", c)
                if b is not None:
                    wait(dve, "pv_done", b)
                    normalise(bank[4], sum_inv, o1, "o1T_done", "o1_recip", "o1_done", b)
                if c is not None:
                    wait(dve, "proj2_done", c)
                    dve.tensor_tensor(h_sb[:, c, :], bank[5][0:T, 0:D], h_sb[:, c, :],
                                      ALU.add).then_inc(S["h2_done"], 1)
                    moments(h_sb[:, c, :], stats2, mean_var2, "h2_done", "stats2_done", "xf_done",
                            "meanvar2_done", c)
                    wait(dve, "rstd2_done", c)
                    wait(dve, "xfT_done", c - 1)
                    dve.tensor_scalar(xf[:], h_sb[:, c, :], mean_var2[:, 0:1], rstd2[:], ALU.subtract,
                                      ALU.mult).then_inc(S["xf_done"], 1)
                if b is not None:
                    wait(dve, "squared", b)
                    wait(dve, "normclamp_done", b - 1)
                    dve.tensor_reduce(norm2[:], squares[:], AX.X, ALU.add).then_inc(S["norm2_done"], 1)
                    wait(dve, "norminv_done", b)
                    wait(dve, "tT_done", b - 1)
                    dve.tensor_tensor(t_tok[:].rearrange("p (h d) -> p h d", h=HEADS),
                                      bank[6][0:T, 0:D].rearrange("p (h d) -> p h d", h=HEADS),
                                      norm_inv[:].unsqueeze(2).to_broadcast([T, HEADS, HD]),
                                      ALU.mult).then_inc(S["t_done"], 1)
                if a is not None:
                    wait(dve, "scores_done", a)
                    wait(dve, "shifted_done", a - 1)
                    for g in range(2):
                        ins = dve.tensor_reduce(row_max[:, g * HG:(g + 1) * HG],
                                                scores_bank[g][0:T, 0:HG * T].rearrange("p (h t) -> p h t", h=HG),
                                                AX.X, ALU.max)
                    ins.then_inc(S["max_done"], 1)
                    wait(dve, "max_done", a)
                    wait(dve, "turned", a - 1)
                    for g in range(2):
                        ins = dve.tensor_tensor(
                            shifted[:, g * HG:(g + 1) * HG, :],
                            scores_bank[g][0:T, 0:HG * T].rearrange("p (h t) -> p h t", h=HG),
                            row_max[:, g * HG:(g + 1) * HG].unsqueeze(2).to_broadcast([T, HG, T]), ALU.subtract)
                    ins.then_inc(S["shifted_done"], 1)

            pipeline(dve, turn)
            wait(dve, "logits_copied", B - 1)
            count = [0]

            def then(ins):
                count[0] += 1
                ins.then_inc(S["d"], 1)
                dve.wait_ge(S["d"], count[0])

            def rank(x, r, n, shape):
                big = [T, shape, n, n]
                xi = x.unsqueeze(3).to_broadcast(big)
                xj = x.unsqueeze(2).to_broadcast(big)
                tie = ties[:, 0:shape, 0:n, 0:n]
                beat = beats[:, 0:shape, 0:n, 0:n]
                then(dve.tensor_tensor(tie, xj, xi, ALU.is_equal))
                then(dve.tensor_tensor(tie, tie, earlier_sb[:, 0:n, 0:n].unsqueeze(1).to_broadcast(big), ALU.mult))
                then(dve.tensor_tensor(beat, xj, xi, ALU.is_gt))
                then(dve.tensor_tensor(beat, beat, tie, ALU.add))
                then(dve.tensor_reduce(r, beat, AX.X, ALU.add))

            def gates(exp, r, k, total, inv, gate, n, shape, exped):
                dve.wait_ge(S[exped], 1)
                then(dve.scalar_tensor_tensor(gate, r, float(k), exp, ALU.is_lt, ALU.mult))
                then(dve.tensor_reduce(total, gate, AX.X, ALU.add))
                then(dve.reciprocal(inv, total))
                then(dve.tensor_tensor(gate, gate, inv.unsqueeze(2).to_broadcast([T, shape, n]), ALU.mult))
                then(dve.scalar_tensor_tensor(gate, gate, GATE_EPS, gate, ALU.is_ge, ALU.mult))

            then(dve.tensor_copy(ex_logits[:].rearrange("p (b g) e -> p b (g e)", b=B), logits[:, :, G:R]))
            then(dve.tensor_reduce(e_max[:], ex_logits[:], AX.X, ALU.max))
            rank(ex_logits[:], e_rank[:], E, B * G)
            then(dve.tensor_tensor(ex_logits[:], ex_logits[:], e_max[:].unsqueeze(2).to_broadcast([T, B * G, E]),
                                   ALU.subtract))
            dve.tensor_copy(e_gate[:, 0:1, 0:1], ex_logits[:, 0:1, 0:1]).then_inc(S["e_ready"], 1)
            then(dve.tensor_reduce(g_max[:], logits[:, :, 0:G], AX.X, ALU.max))
            rank(logits[:, :, 0:G], g_rank[:], G, B)
            dve.tensor_tensor(g_exp[:], logits[:, :, 0:G], g_max[:].unsqueeze(2).to_broadcast([T, B, G]),
                              ALU.subtract).then_inc(S["g_ready"], 1)
            gates(e_exp[:], e_rank[:], KE, e_sum[:], e_inv[:], e_gate[:], E, B * G, "e_exped")
            gates(g_exp[:], g_rank[:], KG, g_sum[:], g_inv[:], g_gate[:], G, B, "g_exped")
            dve.tensor_tensor(combine[:].rearrange("p b (g e) -> p (b g) e", g=G), e_gate[:],
                              g_gate[:].rearrange("p b g -> p (b g)").unsqueeze(2).to_broadcast([T, B * G, E]),
                              ALU.mult).then_inc(S["combine_done"], 1)
            for b in range(B):
                wait(dve, "b2_done", b)
                dve.tensor_tensor(h_sb[:, b, :], bank[2 + b % 2][0:T, 0:D], h_sb[:, b, :],
                                  ALU.add).then_inc(S["y0_done"], 1)
            wait(dve, "y0_done", B - 1)
            dve.wait_ge(S["combine_done"], 1)

            def expert(e):
                for tc in range(4):
                    for j in range(4):
                        b = 4 * tc + j
                        dve.wait_ge(S["g2_done"], e * 16 + b + 1)
                        if not (isinstance(e, int) and e == 0):
                            dve.wait_ge(S["y_done"], (e - 1) * 16 + b + 1)
                        dve.scalar_tensor_tensor(h_sb[:, b, :], bank[4 + j][0:T, 0:D], combine[:, b, bass.ds(e, 1)],
                                                 h_sb[:, b, :], ALU.mult, ALU.add).then_inc(S["y_done"], 1)
            expert(0)
            with dve.Fori(1, NE) as e:
                expert(e)





def kernel(x, txt, L0_tok_W, L0_tok_bias, L0_attn_qkv_w, L0_attn_qkv_b, L0_attn_proj_w, L0_attn_proj_b,
           L0_ffn_Wg, L0_ffn_bg, L0_ffn_We, L0_ffn_be, L0_ffn_W1, L0_ffn_b1, L0_ffn_W2, L0_ffn_b2):
    import numpy as np
    import concourse.bacc as bacc
    from concourse.bass_utils import run_bass_kernel_spmd

    def weight(w, bias):
        w, bias = np.asarray(w), np.asarray(bias)
        rows = np.zeros((HALF + 1, 2, w.shape[1]), w.dtype)
        rows[0:HALF] = w.reshape(2, HALF, -1).transpose(1, 0, 2)
        rows[HALF, 1] = bias
        return rows

    img = np.asarray(x).reshape(B, 3, 6, 16, 6, 16)
    patches = img.transpose(0, 1, 3, 5, 2, 4).reshape(B, PK, 128, PATCH_TOK).transpose(0, 2, 1, 3)
    router = np.concatenate([np.asarray(L0_ffn_Wg),
                             np.asarray(L0_ffn_We).transpose(1, 0, 2).reshape(D, NE)], axis=1)
    router_b = np.concatenate([np.asarray(L0_ffn_bg), np.asarray(L0_ffn_be).reshape(NE)])
    arrays = {
        "patches": patches,
        "tok_w": np.asarray(L0_tok_W).T.reshape(PK, 128, D).transpose(1, 0, 2),
        "tok_b": np.broadcast_to(np.asarray(L0_tok_bias), (PATCH_TOK, D)),
        "txt": np.asarray(txt).transpose(1, 0, 2),
        "qkv_w": weight(np.asarray(L0_attn_qkv_w).T, L0_attn_qkv_b),
        "proj_w": weight(np.asarray(L0_attn_proj_w).T, L0_attn_proj_b),
        "router_w": weight(router, router_b),
        "w1": np.asarray(L0_ffn_W1).reshape(NE, 2, HALF, HID).transpose(0, 2, 1, 3),
        "b1": np.asarray(L0_ffn_b1).reshape(NE, HC, 128).transpose(0, 2, 1),
        "w2": np.asarray(L0_ffn_W2).reshape(NE, HC, 128, D).transpose(0, 2, 1, 3),
        "b2": np.asarray(L0_ffn_b2).reshape(NE, D),
        "identity": np.eye(T, dtype=np.float32),
        "head_mask": np.kron(np.eye(HG, dtype=np.float32), np.ones((HD, 1), np.float32)),
        "earlier": np.broadcast_to(np.tri(E, E, -1, dtype=np.float32), (T, E, E)),
    }
    arrays = {n: np.ascontiguousarray(a) for n, a in arrays.items()}
    nc = bacc.Bacc("TRN2", target_bir_lowering=False, num_devices=1)
    args = {n: nc.dram_tensor(f"in_{n}", a.shape, mybir.dt.from_np(a.dtype), kind="ExternalInput").ap()
            for n, a in arrays.items()}
    out = nc.dram_tensor("out", (T, B, D), F32, kind="ExternalOutput").ap()
    build(nc, out=out, **args)
    result = run_bass_kernel_spmd(nc, [{f"in_{n}": a for n, a in arrays.items()}], core_ids=[0])
    return np.ascontiguousarray(result.results[0]["out"].transpose(1, 0, 2))
```

```python
from contextlib import ExitStack

import concourse.bass as bass
from concourse import mybir

F32 = mybir.dt.float32
I32 = mybir.dt.int32
ALU = mybir.AluOpType
ACT = mybir.ActivationFunctionType
AX = mybir.AxisListType

B = 16
PATCH_TOK = 36
T = 68
D = 192
HALF = 96
HEADS, HD = 12, 16
HG = HEADS // 2
PIX = 768
PK = PIX // 128
G, E = 4, 8
NE = G * E
KG, KE = 2, 4
HID = 768
HC = HID // 128
R = G + NE

TOKENS = B * T
SLOTS = 128
CPE = -(-TOKENS // SLOTS)
TILES = (TOKENS * KG * KE + NE * (SLOTS - 1)) // SLOTS
TILES += -TILES % 4
CHUNKS = 384
assert NE * CPE + TILES - TOKENS * KG * KE // SLOTS <= CHUNKS and TILES <= 128
CONSTANTS = 11
LN_EPS = 1e-5
GATE_EPS = 1e-6
NORM_EPS = 1e-12
ATT_SCALE = HD ** -0.5
SIM_SCALE = 10.0


def build(nc, patches, tok_w, tok_b, txt, qkv_w, proj_w, router_w, w1, b1, w2, b2,
          identity, head_mask, earlier, later_c, region_c, ranks8_c, entries_c, limits_c, tile_no_c,
          ident128_c, blank_c, xf_rows, table, out):
    with ExitStack() as ctx:
        def sb(name, shape):
            return ctx.enter_context(nc.sbuf_tensor(name, shape, F32))

        def sem(name):
            return ctx.enter_context(nc.semaphore(name))

        patches_sb = sb("patches_sb", [128, PK, PATCH_TOK])
        tok_w_sb = sb("tok_w_sb", [128, PK, D])
        tok_b_sb = sb("tok_b_sb", [PATCH_TOK, D])
        qkv_w_sb = sb("qkv_w_sb", [HALF + 1, 2, 3 * D])
        proj_w_sb = sb("proj_w_sb", [HALF + 1, 2, D])
        router_w_sb = sb("router_w_sb", [HALF + 1, 2, R])
        ident = sb("ident", [T, T])
        head_mask_sb = sb("head_mask_sb", [HALF, HG])
        earlier_sb = sb("earlier_sb", [T, E, E])
        eps = sb("eps", [T, 1])
        minus_half = sb("minus_half", [T, HEADS])

        h_sb = sb("h_sb", [T, B, D])
        v_sb = sb("v_sb", [T, B, HEADS, HD + 1])
        xf = sb("xf", [T, D])

        stats = sb("stats", [T, 6])
        mean_var = sb("mean_var", [T, 2])
        var_eps = sb("var_eps", [T, 1])
        rstd = sb("rstd", [T, 1])
        stats2 = sb("stats2", [T, 6])
        mean_var2 = sb("mean_var2", [T, 2])
        var_eps2 = sb("var_eps2", [T, 1])
        rstd2 = sb("rstd2", [T, 1])
        xn = sb("xn", [T, D])
        xn_T = sb("xn_T", [HALF + 1, 2, T])
        qk_T = sb("qk_T", [HALF, 4, T])
        k_wide = sb("k_wide", [HALF, 2, HG, T])
        row_max = sb("row_max", [T, HEADS])
        shifted = sb("shifted", [T, HEADS, T])
        probs_T = sb("probs_T", [T, HEADS, T])
        sum_inv = sb("sum_inv", [T, HEADS])
        o1 = sb("o1", [T, D])
        o1_T = sb("o1_T", [HALF + 1, 2, T])
        squares = sb("squares", [T, HEADS, HD])
        norm2 = sb("norm2", [T, HEADS])
        norm2_clamped = sb("norm2_clamped", [T, HEADS])
        norm_inv = sb("norm_inv", [T, HEADS])
        t_tok = sb("t_tok", [T, D])
        t_T = sb("t_T", [HALF, 2, T])
        t_wide = sb("t_wide", [HALF, 2, HG, T])
        sim_exp = sb("sim_exp", [T, HEADS, T])
        sim_probs = sb("sim_probs", [T, HEADS, T])
        sum2_inv = sb("sum2_inv", [T, HEADS])
        o2 = sb("o2", [T, D])
        o2_T = sb("o2_T", [HALF + 1, 2, T])
        xf_cur = sb("xf_cur", [HALF + 1, 2, T])

        logits = sb("logits", [T, R])
        ties = sb("ties", [T, G, E, E])
        beats = sb("beats", [T, G, E, E])
        g_ties = sb("g_ties", [T, G, G])
        g_beats = sb("g_beats", [T, G, G])
        e_rank = sb("e_rank", [T, G, E])
        g_rank = sb("g_rank", [T, G])
        tops = sb("tops", [T, G + 1])
        below = sb("below", [T, R])
        exps = sb("exps", [T, R])
        e_gate = sb("e_gate", [T, G, E])
        g_gate = sb("g_gate", [T, G])
        gate_sum = sb("gate_sum", [T, G + 1])
        gate_inv = sb("gate_inv", [T, G + 1])
        g_chosen = sb("g_chosen", [T, G])
        chosen = sb("chosen", [T, G, E])
        chosen_before = sb("chosen_before", [T, G, E])
        place = sb("place", [T, G, E])
        e_pick = sb("e_pick", [T, G, KE, E])
        e_work = sb("e_work", [T, G, KE, E])
        e_work2 = sb("e_work2", [T, G, KE, E])
        g_pick = sb("g_pick", [T, KG, G])
        g_work = sb("g_work", [T, KG, G, KE])
        g_work2 = sb("g_work2", [T, KG, G, KE])
        g_share_work = sb("g_share_work", [T, KG, G])
        pick_share = sb("pick_share", [T, KG, KE])
        e_place = sb("e_place", [T, G, KE])
        e_share = sb("e_share", [T, G, KE])
        g_share = sb("g_share", [T, KG])
        pick_place = sb("pick_place", [T, KG, KE])
        places = ctx.enter_context(nc.sbuf_tensor("places", [T, B, KG * KE], I32))
        entries = sb("entries", [T, B, KG * KE, 2])
        ranks8 = sb("ranks8", [T, E])
        region = sb("region", [T, NE])
        later = sb("later", [T, T])
        ones = sb("ones", [T, SLOTS])
        blank = sb("blank", [128, CHUNKS // 128, SLOTS, 2])
        zeros = sb("zeros", [128, D])
        limits = sb("limits", [128, NE, CPE])
        full = sb("full", [128, NE, CPE])
        e_tiles = sb("e_tiles", [128, NE])
        sums = [sb(f"sums{i}", [128, NE]) for i in range(2)]
        passed = sb("passed", [128, NE])
        passed_tiles = sb("passed_tiles", [128, NE])
        tile_no = sb("tile_no", [128, 1])
        tile_expert = sb("tile_expert", [128, 1])
        tile_first = sb("tile_first", [128, 1])
        tile_chunk = sb("tile_chunk", [128, 1])
        chunk_idx = ctx.enter_context(nc.sbuf_tensor("chunk_idx", [128, 1], I32))
        expert_row = ctx.enter_context(nc.sbuf_tensor("expert_row", [1, 128], I32))
        listed = sb("listed", [128, SLOTS, 2])
        ident128 = sb("ident128", [128, 128])
        slot_token = ctx.enter_context(nc.sbuf_tensor("slot_token", [SLOTS, 128], I32))
        slot_gate = sb("slot_gate", [SLOTS, 128])
        w1_sb = [sb(f"w1_sb{i}", [HALF, 2, HID]) for i in range(2)]
        w2_sb = [sb(f"w2_sb{i}", [128, HC, D]) for i in range(2)]
        b1_sb = [sb(f"b1_sb{i}", [128, HC]) for i in range(2)]
        b2_sb = [sb(f"b2_sb{i}", [SLOTS, D]) for i in range(2)]
        x_rows = [sb(f"x_rows{i}", [SLOTS, D]) for i in range(4)]
        x_T = [sb(f"x_T{i}", [HALF, 2, SLOTS]) for i in range(2)]
        hid = [sb(f"hid{i}", [128, HC, SLOTS]) for i in range(2)]
        y_rows = [sb(f"y_rows{i}", [SLOTS, D]) for i in range(2)]
        w1_in = [sem(f"w1_in{i}") for i in range(2)]
        w2_in = [sem(f"w2_in{i}") for i in range(2)]
        b1_in = [sem(f"b1_in{i}") for i in range(2)]
        b2_in = [sem(f"b2_in{i}") for i in range(2)]
        x_in = [sem(f"x_in{i}") for i in range(4)]

        bank = [ctx.enter_context(nc.psum_tensor(f"bank{i}", [128, 512], F32)) for i in range(8)]

        names = """route_exped stored patches_in loaded consts_set mask2_done exp2_done turned scores_exped pv2_done tok_done h_read
        stats_done meanvar_done vareps_done rstd_done xn_done xnT_done xnT_copied o2_recip o2_done o2T_done
        o2T_copied pv_done o1_recip o1_done qk_done v_done proj2_done o1T_done qk_copied v_copied
        o1T_copied h2_done stats2_done meanvar2_done vareps2_done rstd2_done k_wide_done proj1_done
        squared xf_done norm2_done scores_done xfT_done normclamp_done norminv_done t_done tT_done
        xfT_copied tT_copied router_done logits_copied t_wide_done max_done shifted_done sim_done
        rows_out base_out blank_out zeros_out ranked ranking gating choosing below_done gated pos_done place_done picked
        choices_done scattered totals_done listing tiles_listed expert_turned expert_ready chunk_ready
        list_in list_turned list_copied fT_done fT_copied g1_done hid_done g2_done y_added y_done y_out""".split()
        S = {n: sem(n) for n in names}

        loads = [
            (tok_w_sb, tok_w), (tok_b_sb, tok_b), (qkv_w_sb, qkv_w),
            (proj_w_sb, proj_w), (router_w_sb, router_w), (ident, identity),
            (head_mask_sb, head_mask), (earlier_sb, earlier),
            (later, later_c), (region, region_c), (ranks8, ranks8_c), (entries, entries_c),
            (limits, limits_c), (tile_no, tile_no_c), (ident128, ident128_c), (blank, blank_c),
        ]
        loads_done = 16 * (len(loads) + 1)

        def wait(eng, name, b):
            if isinstance(b, int) and b < 0:
                return
            eng.wait_ge(S[name], b + 1)

        def apart(eng):
            eng.wait_ge(S["consts_set"], CONSTANTS)

        def pipeline(eng, body):
            for i in range(5):
                body(i)
            with eng.Fori(5, B) as i:
                body(i)
            for i in range(B, B + 4):
                body(i)

        def stages(i):
            return tuple(i - k if not isinstance(i, int) or 0 <= i - k < B else None for k in range(5))

        scores_bank = [bank[0], bank[1]]
        sim_bank = [bank[2], bank[3]]
        block = ctx.enter_context(nc.Block())

        @block.sync
        def _(sp):
            for dst, src in loads:
                sp.dma_start(dst[:], src).then_inc(S["loaded"], 16)
            sp.dma_start(h_sb[PATCH_TOK:T, :, :], txt).then_inc(S["loaded"], 16)

            sp.wait_ge(S["loaded"], loads_done)
            sp.dma_start(table.rearrange("(p c) w -> p (c w)", p=128), blank[:].rearrange("p c s w -> p (c s w)")
                         ).then_inc(S["blank_out"], 16)
            sp.wait_ge(S["consts_set"], CONSTANTS)
            sp.dma_start(xf_rows[TOKENS:TOKENS + SLOTS, :], zeros[:]).then_inc(S["zeros_out"], 16)
            sp.dma_start(out[TOKENS:TOKENS + SLOTS, :], zeros[:]).then_inc(S["zeros_out"], 16)

            def turn(i):
                a, b, c, _, _ = stages(i)
                if a is not None:
                    wait(sp, "tok_done", a - 1)
                    sp.dma_start(patches_sb[:], patches[a]).then_inc(S["patches_in"], 16)
                if c is not None:
                    wait(sp, "xf_done", c)
                    sp.dma_start(xf_rows[bass.ds(c * T, T), :], xf[:]).then_inc(S["rows_out"], 16)
                    wait(sp, "h2_done", c)
                    sp.dma_start(out[bass.ds(c * T, T), :], h_sb[:, c, :]).then_inc(S["base_out"], 16)

            pipeline(sp, turn)


            def load(e_reg, i, p):
                def free(name, v):
                    if not (isinstance(i, int) and i < 2):
                        sp.wait_ge(S[name], v)
                free("g1_done", HC * (i - 1))
                sp.dma_start(w1_sb[p][:], w1[e_reg]).then_inc(w1_in[p], 16)
                free("hid_done", HC * (i - 1))
                sp.dma_start(b1_sb[p][:], b1[e_reg]).then_inc(b1_in[p], 16)
                free("g2_done", i - 1)
                sp.dma_start(w2_sb[p][:], w2[e_reg]).then_inc(w2_in[p], 16)
                free("y_added", i - 1)
                sp.dma_start(b2_sb[p][:], b2[bass.ds(e_reg, 1), :].to_broadcast([SLOTS, D])).then_inc(b2_in[p], 16)

            sp.wait_ge(S["expert_ready"], 1)

            def expert_of(i):
                return sp.value_load(expert_row[0:1, bass.ds(i, 1)], min_val=0, max_val=NE - 1)
            for i in range(2):
                load(expert_of(i), i, i % 2)
            with sp.Fori(1, TILES // 2) as q:
                for p in range(2):
                    load(expert_of(2 * q + p), 2 * q + p, p)
            sp.wait_ge(S["y_out"], 16 * TILES)

        @block.gpsimd
        def _(pool):
            constants = ([(minus_half[:], -0.5), (eps[:], LN_EPS)]
                         + [(buf[HALF:HALF + 1, :, :], 1.0) for buf in (xn_T, o1_T, o2_T, xf_cur)]
                         + [(v_sb[:, :, :, HD:HD + 1], 1.0), (ones[:], 1.0), (chosen[:], 0.0),
                            (chosen_before[:], 0.0), (zeros[:], 0.0)])
            for n, (dst, value) in enumerate(constants):
                if n > 0:
                    pool.wait_ge(S["consts_set"], n)
                pool.memset(dst, value).then_inc(S["consts_set"], 1)
            pool.wait_ge(S["consts_set"], CONSTANTS)
            pool.wait_ge(S["loaded"], loads_done)

            def inverse_root(mv, tmp, dst, done1, done2, b):
                pool.tensor_tensor(tmp[:], mv[:, 1:2], eps[:], ALU.add).then_inc(S[done1], 1)
                wait(pool, done1, b)
                pool.tensor_tensor(dst[:], tmp[:], minus_half[:, 0:1], ALU.pow).then_inc(S[done2], 1)

            def widen(dst, src, done):
                for g in range(2):
                    ins = pool.tensor_tensor(
                        dst[:, g, :, :], src(g).unsqueeze(1).to_broadcast([HALF, HG, T]),
                        head_mask_sb[:, :].unsqueeze(2).to_broadcast([HALF, HG, T]), ALU.mult)
                ins.then_inc(S[done], 1)

            def turn(i):
                a, b, c, d, f = stages(i)
                if a is not None:
                    wait(pool, "meanvar_done", a)
                    inverse_root(mean_var, var_eps, rstd, "vareps_done", "rstd_done", a)
                if c is not None:
                    wait(pool, "meanvar2_done", c)
                    inverse_root(mean_var2, var_eps2, rstd2, "vareps2_done", "rstd2_done", c)
                if a is not None:
                    wait(pool, "qk_copied", a)
                    wait(pool, "scores_done", a - 1)
                    widen(k_wide, lambda g: qk_T[:, 2 + g, :], "k_wide_done")
                if b is not None:
                    apart(pool)
                    wait(pool, "norm2_done", b)
                    wait(pool, "t_done", b - 1)
                    pool.tensor_scalar(norm2_clamped[:], norm2[:], NORM_EPS ** 2, None,
                                       ALU.max).then_inc(S["normclamp_done"], 1)
                    wait(pool, "normclamp_done", b)
                    pool.tensor_tensor(norm_inv[:], norm2_clamped[:], minus_half[:],
                                       ALU.pow).then_inc(S["norminv_done"], 1)
                    wait(pool, "tT_copied", b)
                    wait(pool, "sim_done", b - 1)
                    widen(t_wide, lambda g: t_T[:, g, :], "t_wide_done")
                if f is not None:
                    wait(pool, "choices_done", f)
                    if f == 0:
                        pool.wait_ge(S["blank_out"], 16)
                    for j in range(KG * KE):
                        pool.indirect_dma_start(
                            out=table, out_offset=bass.IndirectOffsetOnAxis(ap=places[:, f, j:j + 1], axis=0),
                            in_=entries[:, f, j, :], in_offset=None).then_inc(S["scattered"], 16)

            for i in range(B + 4):
                turn(i)

            pool.wait_ge(S["scattered"], 16 * B * KG * KE)
            pool.wait_ge(S["chunk_ready"], 1)
            pool.indirect_dma_start(
                out=listed[:].rearrange("p s w -> p (s w)"), out_offset=None,
                in_=table.rearrange("(c s) w -> c (s w)", s=SLOTS),
                in_offset=bass.IndirectOffsetOnAxis(ap=chunk_idx[:], axis=0)).then_inc(S["list_in"], 16)

            pool.wait_ge(S["rows_out"], 16 * B)
            pool.wait_ge(S["base_out"], 16 * B)
            pool.wait_ge(S["zeros_out"], 32)
            pool.wait_ge(S["list_copied"], 2)
            for i in range(-2, TILES + 1):
                if i + 2 < TILES:
                    if i >= 2:
                        pool.wait_ge(S["fT_done"], i - 1)
                    pool.indirect_dma_start(
                        out=x_rows[(i + 2) % 4][:], out_offset=None, in_=xf_rows,
                        in_offset=bass.IndirectOffsetOnAxis(ap=slot_token[:, i + 2:i + 3], axis=0)
                    ).then_inc(x_in[(i + 2) % 4], 16)
                if i >= 1:
                    pool.wait_ge(S["y_done"], i)
                    if i >= 2:
                        pool.wait_ge(S["y_out"], 16 * (i - 1))
                    pool.indirect_dma_start(
                        out=out, out_offset=bass.IndirectOffsetOnAxis(ap=slot_token[:, i - 1:i], axis=0),
                        in_=y_rows[(i - 1) % 2][:], in_offset=None, compute_op=ALU.add
                    ).then_inc(S["y_out"], 16)

        @block.scalar
        def _(act):
            act.wait_ge(S["consts_set"], CONSTANTS)

            def copy_halves(dst, psum, done):
                act.activation(dst, psum[0:HALF, 0:2 * T].rearrange("p (g t) -> p g t", g=2),
                               ACT.Copy).then_inc(S[done], 1)

            def turn(i):
                a, b, c, d, f = stages(i)
                if c is not None:
                    wait(act, "sim_done", c)
                    wait(act, "mask2_done", c - 1)
                    for g in range(2):
                        ins = act.activation(sim_exp[:, g * HG:(g + 1) * HG, :].rearrange("p h t -> p (h t)"),
                                             sim_bank[g][0:T, 0:HG * T], ACT.Exp, scale=SIM_SCALE)
                    ins.then_inc(S["exp2_done"], 1)
                if b is not None:
                    wait(act, "turned", b)
                    wait(act, "pv_done", b - 1)
                    for g in range(2):
                        ins = act.activation(probs_T[:, g * HG:(g + 1) * HG, :].rearrange("p h t -> p (h t)"),
                                             scores_bank[g][0:T, 0:HG * T], ACT.Exp, scale=ATT_SCALE)
                    ins.then_inc(S["scores_exped"], 1)
                if a is not None:
                    wait(act, "xnT_done", a)
                    wait(act, "v_done", a - 1)
                    copy_halves(xn_T[0:HALF, :, :], bank[7], "xnT_copied")
                if c is not None:
                    wait(act, "o2T_done", c)
                    wait(act, "proj2_done", c - 1)
                    copy_halves(o2_T[0:HALF, :, :], bank[6], "o2T_copied")
                if a is not None:
                    wait(act, "qk_done", a)
                    wait(act, "k_wide_done", a - 1)
                    wait(act, "scores_done", a - 1)
                    act.activation(qk_T[:].rearrange("p q t -> p (q t)"), bank[6][0:HALF, 0:4 * T],
                                   ACT.Copy).then_inc(S["qk_copied"], 1)
                    apart(act)
                    wait(act, "v_done", a)
                    act.activation(v_sb[:, a, :, 0:HD],
                                   bank[7][0:T, 0:D].rearrange("p (h d) -> p h d", h=HEADS),
                                   ACT.Copy).then_inc(S["v_copied"], 1)
                if d is not None:
                    wait(act, "below_done", d)
                    wait(act, "gated", d - 1)
                    act.activation(exps[:], below[:], ACT.Exp).then_inc(S["route_exped"], 1)
                if b is not None:
                    wait(act, "o1T_done", b)
                    wait(act, "proj1_done", b - 1)
                    copy_halves(o1_T[0:HALF, :, :], bank[4], "o1T_copied")
                    wait(act, "proj1_done", b)
                    wait(act, "norm2_done", b - 1)
                    act.activation(squares[:].rearrange("p h d -> p (h d)"), bank[6][0:T, 0:D],
                                   ACT.Square).then_inc(S["squared"], 1)
                if c is not None:
                    wait(act, "xfT_done", c)
                    wait(act, "router_done", c - 1)
                    copy_halves(xf_cur[0:HALF, :, :], bank[5], "xfT_copied")
                if b is not None:
                    wait(act, "tT_done", b)
                    wait(act, "sim_done", b - 1)
                    wait(act, "t_wide_done", b - 1)
                    copy_halves(t_T[:], bank[4], "tT_copied")
                if c is not None:
                    wait(act, "router_done", c)
                    wait(act, "ranked", c - 1)
                    act.activation(logits[:], bank[7][0:T, 0:R], ACT.Copy).then_inc(S["logits_copied"], 1)

            pipeline(act, turn)

            def tile(i, p, turns):
                act.wait_ge(b1_in[p], 16 * turns)
                if not (isinstance(i, int) and i < 2):
                    act.wait_ge(S["g2_done"], i - 1)
                for c in range(HC):
                    act.wait_ge(S["g1_done"], HC * i + c + 1)
                    act.activation(hid[p][:, c, :], bank[(HC * p + c) % 4][:, 0:SLOTS], ACT.Gelu,
                                   bias=b1_sb[p][:, c:c + 1]).then_inc(S["hid_done"], 1)

            for i in range(2):
                tile(i, i, 1)
            with act.Fori(1, TILES // 2) as q:
                for p in range(2):
                    tile(2 * q + p, p, q + 1)

        @block.tensor
        def _(pe):
            pe.wait_ge(S["loaded"], loads_done)
            pe.wait_ge(S["consts_set"], CONSTANTS)

            def turn_halves(psum, src, done):
                for g in range(2):
                    ins = pe.transpose(psum[0:HALF, g * T:(g + 1) * T], src[:, g * HALF:(g + 1) * HALF], ident[:])
                ins.then_inc(S[done], 1)

            def linear(psum, x_T, w, done):
                for g in range(2):
                    k = HALF + g
                    ins = pe.matmul(psum, x_T[0:k, g], w[0:k, g, :], start=(g == 0), stop=(g == 1))
                ins.then_inc(S[done], 1)

            def weighted_values(psum, weights, b, done):
                for h in range(HEADS):
                    ins = pe.matmul(psum[0:T, h * (HD + 1):(h + 1) * (HD + 1)], weights[:, h, :],
                                    v_sb[:, b, h, :], start=True, stop=True)
                ins.then_inc(S[done], 1)

            def turn(i):
                a, b, c, d, f = stages(i)
                if b is not None:
                    wait(pe, "shifted_done", b)
                    for h in range(HEADS):
                        ins = pe.transpose(scores_bank[h // HG][0:T, h % HG * T:(h % HG + 1) * T],
                                           shifted[:, h, :], ident[:])
                    ins.then_inc(S["turned"], 1)
                if c is not None:
                    wait(pe, "mask2_done", c)
                    wait(pe, "tT_copied", c)
                    weighted_values(bank[4], sim_probs, c, "pv2_done")
                if a is not None:
                    wait(pe, "xfT_copied", a - 3)
                    wait(pe, "h_read", a - 1)
                    pe.wait_ge(S["patches_in"], 16 * (a + 1))
                    for k in range(PK):
                        ins = pe.matmul(bank[5][0:PATCH_TOK, 0:D], patches_sb[:, k, :] if isinstance(a, int)
                                        else patches_sb[:, k, :], tok_w_sb[:, k, :],
                                        start=(k == 0), stop=(k == PK - 1))
                    ins.then_inc(S["tok_done"], 1)
                    wait(pe, "xn_done", a)
                    wait(pe, "place_done", a - 4)
                    wait(pe, "logits_copied", a - 3)
                    wait(pe, "v_copied", a - 1)
                    turn_halves(bank[7], xn, "xnT_done")
                if c is not None:
                    wait(pe, "o2_done", c)
                    wait(pe, "t_done", c)
                    turn_halves(bank[6], o2, "o2T_done")
                if b is not None:
                    wait(pe, "scores_exped", b)
                    wait(pe, "tT_copied", b - 1)
                    if c is not None:
                        wait(pe, "o2_done", c)
                    weighted_values(bank[4], probs_T, b, "pv_done")
                if a is not None:
                    wait(pe, "xnT_copied", a)
                    if c is not None:
                        wait(pe, "o2T_copied", c)
                    for q in range(4):
                        for g in range(2):
                            k = HALF + g
                            ins = pe.matmul(bank[6][0:HALF, q * T:(q + 1) * T],
                                            qkv_w_sb[0:k, g, q * HALF:(q + 1) * HALF], xn_T[0:k, g, :],
                                            start=(g == 0), stop=(g == 1))
                    ins.then_inc(S["qk_done"], 1)
                    linear(bank[7][0:T, 0:D], xn_T, qkv_w_sb[:, :, 2 * D:3 * D], "v_done")
                if c is not None:
                    wait(pe, "o2T_copied", c)
                    if a is not None:
                        wait(pe, "h_read", a)
                    linear(bank[5][0:T, 0:D], o2_T, proj_w_sb, "proj2_done")
                if b is not None:
                    wait(pe, "o1_done", b)
                    turn_halves(bank[4], o1, "o1T_done")
                    wait(pe, "o1T_copied", b)
                    if a is not None:
                        wait(pe, "qk_copied", a)
                    linear(bank[6][0:T, 0:D], o1_T, proj_w_sb, "proj1_done")
                if a is not None:
                    wait(pe, "k_wide_done", a)
                    if b is not None:
                        wait(pe, "scores_exped", b)
                    for g in range(2):
                        ins = pe.matmul(scores_bank[g][0:T, 0:HG * T], qk_T[:, g, :],
                                        k_wide[:, g, :, :].rearrange("p h t -> p (h t)"), start=True, stop=True)
                    ins.then_inc(S["scores_done"], 1)
                if c is not None:
                    wait(pe, "xf_done", c)
                    turn_halves(bank[5], xf, "xfT_done")
                if b is not None:
                    wait(pe, "t_done", b)
                    turn_halves(bank[4], t_tok, "tT_done")
                if c is not None:
                    wait(pe, "xfT_copied", c)
                    wait(pe, "logits_copied", c - 1)
                    wait(pe, "place_done", c - 2)
                    if a is not None:
                        wait(pe, "v_copied", a)
                    linear(bank[7][0:T, 0:R], xf_cur, router_w_sb, "router_done")
                if b is not None:
                    wait(pe, "t_wide_done", b)
                    wait(pe, "mask2_done", b - 1)
                    for g in range(2):
                        ins = pe.matmul(sim_bank[g][0:T, 0:HG * T], t_T[:, g, :],
                                        t_wide[:, g, :, :].rearrange("p h t -> p (h t)"), start=True, stop=True)
                    ins.then_inc(S["sim_done"], 1)
                if d is not None:
                    wait(pe, "ranked", d)
                    if c is not None:
                        wait(pe, "logits_copied", c)
                    wait(pe, "place_done", d - 1)
                    pe.matmul(bank[7][0:T, 0:NE], later[:], chosen[:].rearrange("p g e -> p (g e)"),
                              start=True, stop=False)
                    pe.matmul(bank[7][0:T, 0:NE], ones[:, 0:T], chosen_before[:].rearrange("p g e -> p (g e)"),
                              start=False, stop=True).then_inc(S["pos_done"], 1)

            pipeline(pe, turn)

            wait(pe, "ranked", B - 1)
            wait(pe, "t_done", B - 1)
            pe.matmul(bank[6][:, 0:NE], ones[:], chosen[:].rearrange("p g e -> p (g e)"), start=True, stop=False)
            pe.matmul(bank[6][:, 0:NE], ones[:], chosen_before[:].rearrange("p g e -> p (g e)"), start=False,
                      stop=True).then_inc(S["totals_done"], 1)
            pe.wait_ge(S["tiles_listed"], 1)
            pe.transpose(bank[5][0:1, 0:128], tile_expert[:], ident128[:]).then_inc(S["expert_turned"], 1)
            pe.wait_ge(S["list_in"], 16)
            for w in range(2):
                pe.transpose(bank[w][0:SLOTS, 0:128], listed[:, :, w], ident128[:]).then_inc(S["list_turned"], 1)
            pe.wait_ge(S["list_copied"], 2)

            def turn_x(i, r):
                pe.wait_ge(x_in[r[0]], 16 * r[1])
                if not (isinstance(i, int) and i < 2):
                    pe.wait_ge(S["fT_copied"], i - 1)
                for g in range(2):
                    ins = pe.transpose(bank[6 + r[0] % 2][0:HALF, g * SLOTS:(g + 1) * SLOTS],
                                       x_rows[r[0]][:, g * HALF:(g + 1) * HALF], ident128[:])
                ins.then_inc(S["fT_done"], 1)

            def up(i, p, turns):
                pe.wait_ge(S["fT_copied"], i + 1)
                pe.wait_ge(w1_in[p], 16 * turns)
                for c in range(HC):
                    if not (isinstance(i, int) and HC * i + c < 4):
                        pe.wait_ge(S["hid_done"], HC * i + c - 3)
                    for g in range(2):
                        ins = pe.matmul(bank[(HC * p + c) % 4][:, 0:SLOTS], w1_sb[p][:, g, c * 128:(c + 1) * 128],
                                        x_T[p][:, g, :], start=(g == 0), stop=(g == 1))
                    ins.then_inc(S["g1_done"], 1)

            def down(i, p, turns):
                pe.wait_ge(S["hid_done"], HC * (i + 1))
                pe.wait_ge(w2_in[p], 16 * turns)
                if not (isinstance(i, int) and i < 2):
                    pe.wait_ge(S["y_added"], i - 1)
                for c in range(HC):
                    ins = pe.matmul(bank[4 + p][0:SLOTS, 0:D], hid[p][:, c, :], w2_sb[p][:, c, :],
                                    start=(c == 0), stop=(c == HC - 1))
                ins.then_inc(S["g2_done"], 1)

            turn_x(0, (0, 1))
            def four(q, first, last):
                for r in range(4):
                    i = 4 * q + r
                    if not (last and r == 3):
                        turn_x(i + 1, ((r + 1) % 4, q + 1 + (r == 3)))
                    up(i, r % 2, 2 * q + r // 2 + 1)
                    if not (first and r == 0):
                        down(i - 1, (r + 1) % 2, 2 * q + (r + 1) // 2)
            four(0, True, False)
            with pe.Fori(1, TILES // 4 - 1) as q:
                four(q, False, False)
            four(TILES // 4 - 1, False, True)
            down(TILES - 1, 1, TILES // 2)

        @block.vector
        def _(dve):
            dve.wait_ge(S["loaded"], loads_done)
            dve.wait_ge(S["consts_set"], CONSTANTS)

            def by_head(psum):
                return psum[0:T, 0:HEADS * (HD + 1)].rearrange("p (h d) -> p h d", h=HEADS)

            def normalise(psum, inv, dst, free, recip, done, b):
                pv = by_head(psum)
                wait(dve, done, b - 1)
                dve.reciprocal(inv[:].unsqueeze(2), pv[:, :, HD:HD + 1]).then_inc(S[recip], 1)
                wait(dve, recip, b)
                wait(dve, free, b - 1)
                dve.tensor_tensor(dst[:].rearrange("p (h d) -> p h d", h=HEADS), pv[:, :, 0:HD],
                                  inv[:].unsqueeze(2).to_broadcast([T, HEADS, HD]), ALU.mult).then_inc(S[done], 1)

            def moments(src, st, mv, h_ready, st_done, free, done, b):
                apart(dve)
                wait(dve, h_ready, b)
                wait(dve, done, b - 1)
                dve.bn_stats(st[:], src).then_inc(S[st_done], 1)
                apart(dve)
                wait(dve, st_done, b)
                wait(dve, free, b - 1)
                dve.bn_aggr(mv[:], st[:]).then_inc(S[done], 1)

            def chain(b, total, name):
                n = [0]

                def then(ins):
                    n[0] += 1
                    ins.then_inc(S[name], 1)
                    dve.wait_ge(S[name], total * b + n[0])
                    assert n[0] <= total
                return then

            e_flat = "p g e -> p (g e)"

            def ranks(d):
                then = chain(d, 7, "ranking")
                wait(dve, "logits_copied", d)
                e_logits = logits[:, G:R].rearrange("p (g e) -> p g e", g=G)
                dve.tensor_reduce(tops[:, 0:G], e_logits, AX.X, ALU.max)
                then(dve.tensor_reduce(tops[:, G:G + 1], logits[:, 0:G], AX.X, ALU.max))
                wait(dve, "route_exped", d - 1)
                dve.tensor_tensor(below[:, G:R].rearrange("p (g e) -> p g e", g=G), e_logits,
                                  tops[:, 0:G].unsqueeze(2).to_broadcast([T, G, E]), ALU.subtract)
                dve.tensor_scalar(below[:, 0:G], logits[:, 0:G], tops[:, G:G + 1], None,
                                  ALU.subtract).then_inc(S["below_done"], 1)
                four, three = [T, G, E, E], [T, G, G]
                ei, ej = e_logits.unsqueeze(3).to_broadcast(four), e_logits.unsqueeze(2).to_broadcast(four)
                gi = logits[:, 0:G].unsqueeze(2).to_broadcast(three)
                gj = logits[:, 0:G].unsqueeze(1).to_broadcast(three)
                dve.tensor_tensor(ties[:], ej, ei, ALU.is_equal)
                dve.tensor_tensor(g_ties[:], gj, gi, ALU.is_equal)
                dve.tensor_tensor(beats[:], ej, ei, ALU.is_gt)
                then(dve.tensor_tensor(g_beats[:], gj, gi, ALU.is_gt))
                dve.tensor_tensor(ties[:], ties[:], earlier_sb[:].unsqueeze(1).to_broadcast(four), ALU.mult)
                then(dve.tensor_tensor(g_ties[:], g_ties[:], earlier_sb[:, 0:G, 0:G], ALU.mult))
                dve.tensor_tensor(beats[:], beats[:], ties[:], ALU.add)
                then(dve.tensor_tensor(g_beats[:], g_beats[:], g_ties[:], ALU.add))
                dve.tensor_reduce(e_rank[:], beats[:], AX.X, ALU.add)
                then(dve.tensor_reduce(g_rank[:], g_beats[:], AX.X, ALU.add))
                dve.tensor_scalar(g_chosen[:], g_rank[:], float(KG), None, ALU.is_lt)
                wait(dve, "pos_done", d - 1)
                then(dve.tensor_tensor(chosen_before[:], chosen_before[:], chosen[:], ALU.add))
                then(dve.tensor_scalar(chosen[:].rearrange(e_flat), e_rank[:].rearrange(e_flat), float(KE), None,
                                       ALU.is_lt))
                dve.tensor_tensor(chosen[:], chosen[:], g_chosen[:].unsqueeze(2).to_broadcast([T, G, E]),
                                  ALU.mult).then_inc(S["ranked"], 1)

            def gates(d):
                then = chain(d, 4, "gating")
                wait(dve, "route_exped", d)
                dve.scalar_tensor_tensor(e_gate[:].rearrange(e_flat), e_rank[:].rearrange(e_flat), float(KE),
                                         exps[:, G:R], ALU.is_lt, ALU.mult)
                then(dve.scalar_tensor_tensor(g_gate[:], g_rank[:], float(KG), exps[:, 0:G], ALU.is_lt, ALU.mult))
                dve.tensor_reduce(gate_sum[:, 0:G], e_gate[:], AX.X, ALU.add)
                then(dve.tensor_reduce(gate_sum[:, G:G + 1], g_gate[:], AX.X, ALU.add))
                then(dve.reciprocal(gate_inv[:], gate_sum[:]))
                dve.tensor_tensor(e_gate[:], e_gate[:], gate_inv[:, 0:G].unsqueeze(2).to_broadcast([T, G, E]),
                                  ALU.mult)
                then(dve.tensor_scalar(g_gate[:], g_gate[:], gate_inv[:, G:G + 1], None, ALU.mult))
                dve.scalar_tensor_tensor(e_gate[:].rearrange(e_flat), e_gate[:].rearrange(e_flat), GATE_EPS,
                                         e_gate[:].rearrange(e_flat), ALU.is_ge, ALU.mult)
                dve.scalar_tensor_tensor(g_gate[:], g_gate[:], GATE_EPS, g_gate[:], ALU.is_ge,
                                         ALU.mult).then_inc(S["gated"], 1)

            def choices(f):
                then = chain(f, 5, "choosing")
                wide = [T, G, KE, E]
                mid = [T, KG, G, KE]
                wait(dve, "place_done", f)
                wait(dve, "gated", f)
                dve.tensor_tensor(e_pick[:], e_rank[:].unsqueeze(2).to_broadcast(wide),
                                  ranks8[:, 0:KE].unsqueeze(1).unsqueeze(3).to_broadcast(wide), ALU.is_equal)
                then(dve.tensor_tensor(g_pick[:], g_rank[:].unsqueeze(1).to_broadcast([T, KG, G]),
                                       ranks8[:, 0:KG].unsqueeze(2).to_broadcast([T, KG, G]), ALU.is_equal))
                dve.tensor_tensor(e_work[:], e_pick[:], place[:].unsqueeze(2).to_broadcast(wide), ALU.mult)
                dve.tensor_tensor(g_share_work[:], g_pick[:], g_gate[:].unsqueeze(1).to_broadcast([T, KG, G]),
                                  ALU.mult)
                then(dve.tensor_tensor(e_work2[:], e_pick[:], e_gate[:].unsqueeze(2).to_broadcast(wide), ALU.mult))
                dve.tensor_reduce(e_place[:], e_work[:], AX.X, ALU.add)
                dve.tensor_reduce(g_share[:], g_share_work[:], AX.X, ALU.add)
                then(dve.tensor_reduce(e_share[:], e_work2[:], AX.X, ALU.add))
                dve.tensor_tensor(g_work[:], g_pick[:].unsqueeze(3).to_broadcast(mid),
                                  e_place[:].unsqueeze(1).to_broadcast(mid), ALU.mult)
                then(dve.tensor_tensor(g_work2[:], g_pick[:].unsqueeze(3).to_broadcast(mid),
                                       e_share[:].unsqueeze(1).to_broadcast(mid), ALU.mult))
                dve.tensor_reduce(pick_place[:], g_work[:].rearrange("p r g k -> p r k g"), AX.X, ALU.add)
                then(dve.tensor_reduce(pick_share[:], g_work2[:].rearrange("p r g k -> p r k g"), AX.X, ALU.add))
                dve.tensor_scalar(places[:, f, :], pick_place[:].rearrange("p r k -> p (r k)"), 0.0, None, ALU.add)
                dve.tensor_tensor(entries[:, f, :, 1].rearrange("p (r k) -> p r k", r=KG), pick_share[:],
                                  g_share[:].unsqueeze(2).to_broadcast([T, KG, KE]),
                                  ALU.mult).then_inc(S["choices_done"], 1)

            def turn(i):
                a, b, c, d, f = stages(i)
                if c is not None:
                    wait(dve, "exp2_done", c)
                    wait(dve, "pv2_done", c - 1)
                    for g in range(2):
                        ins = dve.scalar_tensor_tensor(
                            sim_probs[:, g * HG:(g + 1) * HG, :].rearrange("p h t -> p (h t)"),
                            sim_bank[g][0:T, 0:HG * T], 0.0,
                            sim_exp[:, g * HG:(g + 1) * HG, :].rearrange("p h t -> p (h t)"), ALU.is_ge, ALU.mult)
                    ins.then_inc(S["mask2_done"], 1)
                if f is not None:
                    wait(dve, "pos_done", f)
                    dve.tensor_tensor(place[:].rearrange("p g e -> p (g e)"), bank[7][0:T, 0:NE], region[:],
                                      ALU.add).then_inc(S["place_done"], 1)
                if a is not None:
                    wait(dve, "tok_done", a)
                    dve.tensor_tensor(h_sb[0:PATCH_TOK, a, :], bank[5][0:PATCH_TOK, 0:D], tok_b_sb[:],
                                      ALU.add).then_inc(S["h_read"], 1)
                    moments(h_sb[:, a, :], stats, mean_var, "h_read", "stats_done", "xn_done", "meanvar_done", a)
                    wait(dve, "rstd_done", a)
                    wait(dve, "xnT_done", a - 1)
                    dve.tensor_scalar(xn[:], h_sb[:, a, :], mean_var[:, 0:1], rstd[:], ALU.subtract,
                                      ALU.mult).then_inc(S["xn_done"], 1)
                if c is not None:
                    wait(dve, "pv2_done", c)
                    normalise(bank[4], sum2_inv, o2, "o2T_done", "o2_recip", "o2_done", c)
                if b is not None:
                    wait(dve, "pv_done", b)
                    normalise(bank[4], sum_inv, o1, "o1T_done", "o1_recip", "o1_done", b)
                if f is not None:
                    choices(f)
                if d is not None:
                    ranks(d)
                if c is not None:
                    wait(dve, "proj2_done", c)
                    dve.tensor_tensor(h_sb[:, c, :], bank[5][0:T, 0:D], h_sb[:, c, :],
                                      ALU.add).then_inc(S["h2_done"], 1)
                    moments(h_sb[:, c, :], stats2, mean_var2, "h2_done", "stats2_done", "xf_done",
                            "meanvar2_done", c)
                    wait(dve, "rstd2_done", c)
                    if not (isinstance(c, int) and c == 0):
                        dve.wait_ge(S["rows_out"], 16 * c)
                    dve.tensor_scalar(xf[:], h_sb[:, c, :], mean_var2[:, 0:1], rstd2[:], ALU.subtract,
                                      ALU.mult).then_inc(S["xf_done"], 1)
                if b is not None:
                    wait(dve, "squared", b)
                    wait(dve, "normclamp_done", b - 1)
                    dve.tensor_reduce(norm2[:], squares[:], AX.X, ALU.add).then_inc(S["norm2_done"], 1)
                    wait(dve, "norminv_done", b)
                    wait(dve, "tT_done", b - 1)
                    dve.tensor_tensor(t_tok[:].rearrange("p (h d) -> p h d", h=HEADS),
                                      bank[6][0:T, 0:D].rearrange("p (h d) -> p h d", h=HEADS),
                                      norm_inv[:].unsqueeze(2).to_broadcast([T, HEADS, HD]),
                                      ALU.mult).then_inc(S["t_done"], 1)
                if d is not None:
                    gates(d)
                if a is not None:
                    wait(dve, "scores_done", a)
                    wait(dve, "shifted_done", a - 1)
                    for g in range(2):
                        ins = dve.tensor_reduce(row_max[:, g * HG:(g + 1) * HG],
                                                scores_bank[g][0:T, 0:HG * T].rearrange("p (h t) -> p h t", h=HG),
                                                AX.X, ALU.max)
                    ins.then_inc(S["max_done"], 1)
                    wait(dve, "max_done", a)
                    wait(dve, "turned", a - 1)
                    for g in range(2):
                        ins = dve.tensor_tensor(
                            shifted[:, g * HG:(g + 1) * HG, :],
                            scores_bank[g][0:T, 0:HG * T].rearrange("p (h t) -> p h t", h=HG),
                            row_max[:, g * HG:(g + 1) * HG].unsqueeze(2).to_broadcast([T, HG, T]), ALU.subtract)
                    ins.then_inc(S["shifted_done"], 1)

            pipeline(dve, turn)
            count = [0]

            def then(ins):
                count[0] += 1
                ins.then_inc(S["listing"], 1)
                dve.wait_ge(S["listing"], count[0])

            dve.wait_ge(S["totals_done"], 1)
            totals = bank[6][:, 0:NE].unsqueeze(2).to_broadcast([128, NE, CPE])
            then(dve.tensor_tensor(full[:], totals, limits[:], ALU.is_gt))
            then(dve.tensor_reduce(e_tiles[:], full[:], AX.X, ALU.add))
            src, n = e_tiles, 0
            for step in (1, 2, 4, 8, 16):
                dst = sums[n % 2]
                dve.tensor_copy(dst[:, 0:step], src[:, 0:step])
                then(dve.tensor_tensor(dst[:, step:NE], src[:, step:NE], src[:, 0:NE - step], ALU.add))
                src, n = dst, n + 1
            then(dve.tensor_scalar(passed[:], src[:], tile_no[:], None, ALU.is_le))
            dve.tensor_tensor(passed_tiles[:], passed[:], e_tiles[:], ALU.mult)
            then(dve.tensor_reduce(tile_expert[:], passed[:], AX.X, ALU.add))
            then(dve.tensor_reduce(tile_first[:], passed_tiles[:], AX.X, ALU.add))
            then(dve.scalar_tensor_tensor(tile_chunk[:], tile_expert[:], float(CPE), tile_no[:], ALU.mult, ALU.add))
            dve.tensor_tensor(chunk_idx[:], tile_chunk[:], tile_first[:], ALU.subtract
                              ).then_inc(S["chunk_ready"], 1)
            dve.tensor_scalar(tile_expert[:], tile_expert[:], float(NE - 1), None, ALU.min
                              ).then_inc(S["tiles_listed"], 1)
            dve.wait_ge(S["expert_turned"], 1)
            dve.tensor_copy(expert_row[:], bank[5][0:1, 0:128]).then_inc(S["expert_ready"], 1)
            for w, dst in enumerate((slot_token, slot_gate)):
                dve.wait_ge(S["list_turned"], w + 1)
                dve.tensor_copy(dst[:], bank[w][0:SLOTS, 0:128]).then_inc(S["list_copied"], 1)

            def copy_x(i, p):
                dve.wait_ge(S["fT_done"], i + 1)
                if not (isinstance(i, int) and i < 2):
                    dve.wait_ge(S["g1_done"], HC * (i - 1))
                dve.tensor_copy(x_T[p][:].rearrange("p g s -> p (g s)"), bank[6 + p][0:HALF, 0:2 * SLOTS]
                                ).then_inc(S["fT_copied"], 1)

            def weigh(i, p, turns):
                dve.wait_ge(S["g2_done"], i + 1)
                dve.wait_ge(b2_in[p], 16 * turns)
                if not (isinstance(i, int) and i < 2):
                    dve.wait_ge(S["y_out"], 16 * (i - 1))
                dve.tensor_tensor(y_rows[p][:], bank[4 + p][0:SLOTS, 0:D], b2_sb[p][:],
                                  ALU.add).then_inc(S["y_added"], 1)
                dve.wait_ge(S["y_added"], i + 1)
                dve.tensor_scalar(y_rows[p][:], y_rows[p][:], slot_gate[:, bass.ds(i, 1)], None,
                                  ALU.mult).then_inc(S["y_done"], 1)

            def two(q, first, last):
                for p in range(2):
                    i = 2 * q + p
                    if not (last and p == 1):
                        copy_x(i + 1, (p + 1) % 2)
                    if not (first and p == 0):
                        weigh(i - 1, (p + 1) % 2, q + p)
            copy_x(0, 0)
            two(0, True, False)
            with dve.Fori(1, TILES // 2 - 1) as q:
                two(q, False, False)
            two(TILES // 2 - 1, False, True)
            weigh(TILES - 1, 1, TILES // 2)


def kernel(x, txt, L0_tok_W, L0_tok_bias, L0_attn_qkv_w, L0_attn_qkv_b, L0_attn_proj_w, L0_attn_proj_b,
           L0_ffn_Wg, L0_ffn_bg, L0_ffn_We, L0_ffn_be, L0_ffn_W1, L0_ffn_b1, L0_ffn_W2, L0_ffn_b2):
    import numpy as np
    import concourse.bacc as bacc
    from concourse.bass_utils import run_bass_kernel_spmd

    def weight(w, bias):
        w, bias = np.asarray(w), np.asarray(bias)
        rows = np.zeros((HALF + 1, 2, w.shape[1]), w.dtype)
        rows[0:HALF] = w.reshape(2, HALF, -1).transpose(1, 0, 2)
        rows[HALF, 1] = bias
        return rows

    img = np.asarray(x).reshape(B, 3, 6, 16, 6, 16)
    patches = img.transpose(0, 1, 3, 5, 2, 4).reshape(B, PK, 128, PATCH_TOK).transpose(0, 2, 1, 3)
    router = np.concatenate([np.asarray(L0_ffn_Wg),
                             np.asarray(L0_ffn_We).transpose(1, 0, 2).reshape(D, NE)], axis=1)
    router_b = np.concatenate([np.asarray(L0_ffn_bg), np.asarray(L0_ffn_be).reshape(NE)])
    entries = np.zeros((T, B, KG * KE, 2), np.float32)
    entries[..., 0] = (np.arange(B) * T + np.arange(T)[:, None])[..., None]
    blank = np.zeros((128, CHUNKS // 128, SLOTS, 2), np.float32)
    blank[..., 0] = TOKENS + np.arange(SLOTS)
    arrays = {
        "patches": patches,
        "tok_w": np.asarray(L0_tok_W).T.reshape(PK, 128, D).transpose(1, 0, 2),
        "tok_b": np.broadcast_to(np.asarray(L0_tok_bias), (PATCH_TOK, D)),
        "txt": np.asarray(txt).transpose(1, 0, 2),
        "qkv_w": weight(np.asarray(L0_attn_qkv_w).T, L0_attn_qkv_b),
        "proj_w": weight(np.asarray(L0_attn_proj_w).T, L0_attn_proj_b),
        "router_w": weight(router, router_b),
        "w1": np.asarray(L0_ffn_W1).reshape(NE, 2, HALF, HID).transpose(0, 2, 1, 3),
        "b1": np.asarray(L0_ffn_b1).reshape(NE, HC, 128).transpose(0, 2, 1),
        "w2": np.asarray(L0_ffn_W2).reshape(NE, HC, 128, D).transpose(0, 2, 1, 3),
        "b2": np.asarray(L0_ffn_b2).reshape(NE, D),
        "identity": np.eye(T, dtype=np.float32),
        "head_mask": np.kron(np.eye(HG, dtype=np.float32), np.ones((HD, 1), np.float32)),
        "earlier": np.broadcast_to(np.tri(E, E, -1, dtype=np.float32), (T, E, E)),
        "later_c": np.tri(T, T, -1, dtype=np.float32).T,
        "region_c": np.broadcast_to(np.arange(NE, dtype=np.float32) * CPE * SLOTS, (T, NE)),
        "ranks8_c": np.broadcast_to(np.arange(E, dtype=np.float32), (T, E)),
        "entries_c": entries,
        "limits_c": np.broadcast_to(np.arange(CPE, dtype=np.float32) * SLOTS, (128, NE, CPE)),
        "tile_no_c": np.arange(128, dtype=np.float32)[:, None],
        "ident128_c": np.eye(128, dtype=np.float32),
        "blank_c": blank,
    }
    arrays = {n: np.ascontiguousarray(a) for n, a in arrays.items()}
    nc = bacc.Bacc("TRN2", target_bir_lowering=False, num_devices=1)
    args = {n: nc.dram_tensor(f"in_{n}", a.shape, mybir.dt.from_np(a.dtype), kind="ExternalInput").ap()
            for n, a in arrays.items()}
    xf_rows = nc.dram_tensor("xf_rows", (TOKENS + SLOTS, D), F32, kind="Internal").ap()
    table = nc.dram_tensor("table", (CHUNKS * SLOTS, 2), F32, kind="Internal").ap()
    out = nc.dram_tensor("out", (TOKENS + SLOTS, D), F32, kind="ExternalOutput").ap()
    build(nc, xf_rows=xf_rows, table=table, out=out, **args)
    result = run_bass_kernel_spmd(nc, [{f"in_{n}": a for n, a in arrays.items()}], core_ids=[0])
    return np.ascontiguousarray(result.results[0]["out"][0:TOKENS].reshape(B, T, D))
```

```python
from contextlib import ExitStack

import concourse.bass as bass
from concourse import mybir

F32 = mybir.dt.float32
I32 = mybir.dt.int32
ALU = mybir.AluOpType
ACT = mybir.ActivationFunctionType
AX = mybir.AxisListType

B = 16
PATCH_TOK = 36
T = 68
D = 192
HALF = 96
HEADS, HD = 12, 16
HG = HEADS // 2
PIX = 768
PK = PIX // 128
G, E = 4, 8
NE = G * E
KG, KE = 2, 4
HID = 768
HC = HID // 128
R = G + NE

GROUP = 3
GROUPS = -(-B // GROUP)
GROUP_ROWS = GROUP * PATCH_TOK

TOKENS = B * T
SLOTS = 128
CPE = -(-TOKENS // SLOTS)
TILES = (TOKENS * KG * KE + NE * (SLOTS - 1)) // SLOTS
X_BUFS = 4
TILES += -TILES % X_BUFS
CHUNKS = 384
SURE = TOKENS * KG * KE // SLOTS // X_BUFS * X_BUFS
SPARE_GROUPS = (TILES - SURE) // X_BUFS
assert NE * CPE + 128 - TOKENS * KG * KE // SLOTS <= CHUNKS and TILES < 128 and SURE % X_BUFS == 0
CONSTANTS = 11
LN_EPS = 1e-5
GATE_EPS = 1e-6
NORM_EPS = 1e-12
ATT_SCALE = HD ** -0.5
SIM_SCALE = 10.0


def build(nc, patches, tok_w, tok_b, txt, qkv_w, proj_w, router_w, w1, b1, w2, b2,
          identity, head_mask, earlier, later_c, region_c, ranks8_c, entries_c, limits_c, tile_no_c,
          ident128_c, group_first_c, blank_c, xf_rows, table, out):
    with ExitStack() as ctx:
        def sb(name, shape):
            return ctx.enter_context(nc.sbuf_tensor(name, shape, F32))

        def sem(name):
            return ctx.enter_context(nc.semaphore(name))

        patches_sb = sb("patches_sb", [128, GROUPS, PK, GROUP_ROWS])
        tok_w_sb = sb("tok_w_sb", [128, PK, D])
        tok_b_sb = sb("tok_b_sb", [GROUP_ROWS, D])
        embedded = sb("embedded", [GROUP_ROWS, GROUPS, D])
        qkv_w_sb = sb("qkv_w_sb", [HALF + 1, 2, 3 * D])
        proj_w_sb = sb("proj_w_sb", [HALF + 1, 2, D])
        router_w_sb = sb("router_w_sb", [HALF + 1, 2, R])
        ident = sb("ident", [T, T])
        head_mask_sb = sb("head_mask_sb", [HALF, HG])
        earlier_sb = sb("earlier_sb", [T, E, E])
        eps = sb("eps", [T, 1])
        minus_half = sb("minus_half", [T, HEADS])

        h_sb = sb("h_sb", [T, B, D])
        v_sb = sb("v_sb", [T, B, HEADS, HD + 1])
        xf = sb("xf", [T, D])

        stats = sb("stats", [T, 6])
        mean_var = sb("mean_var", [T, 2])
        var_eps = sb("var_eps", [T, 1])
        rstd = sb("rstd", [T, 1])
        stats2 = sb("stats2", [T, 6])
        mean_var2 = sb("mean_var2", [T, 2])
        var_eps2 = sb("var_eps2", [T, 1])
        rstd2 = sb("rstd2", [T, 1])
        xn = sb("xn", [T, D])
        xn_T = sb("xn_T", [HALF + 1, 2, T])
        qk_T = sb("qk_T", [HALF, 4, T])
        k_wide = sb("k_wide", [HALF, 2, HG, T])
        row_max = sb("row_max", [T, HEADS])
        shifted = sb("shifted", [T, HEADS, T])
        probs_T = sb("probs_T", [T, HEADS, T])
        sum_inv = sb("sum_inv", [T, HEADS])
        o1 = sb("o1", [T, D])
        o1_T = sb("o1_T", [HALF + 1, 2, T])
        squares = sb("squares", [T, HEADS, HD])
        norm2 = sb("norm2", [T, HEADS])
        norm2_clamped = sb("norm2_clamped", [T, HEADS])
        norm_inv = sb("norm_inv", [T, HEADS])
        t_tok = sb("t_tok", [T, D])
        t_T = sb("t_T", [HALF, 2, T])
        t_wide = sb("t_wide", [HALF, 2, HG, T])
        sim_exp = sb("sim_exp", [T, HEADS, T])
        sim_probs = sb("sim_probs", [T, HEADS, T])
        sum2_inv = sb("sum2_inv", [T, HEADS])
        o2 = sb("o2", [T, D])
        o2_T = sb("o2_T", [HALF + 1, 2, T])
        xf_cur = sb("xf_cur", [HALF + 1, 2, T])

        logits = sb("logits", [T, R])
        ties = sb("ties", [T, G, E, E])
        beats = sb("beats", [T, G, E, E])
        g_ties = sb("g_ties", [T, G, G])
        g_beats = sb("g_beats", [T, G, G])
        e_rank = sb("e_rank", [T, G, E])
        g_rank = sb("g_rank", [T, G])
        tops = sb("tops", [T, G + 1])
        below = sb("below", [T, R])
        exps = sb("exps", [T, R])
        e_gate = sb("e_gate", [T, G, E])
        g_gate = sb("g_gate", [T, G])
        gate_sum = sb("gate_sum", [T, G + 1])
        gate_inv = sb("gate_inv", [T, G + 1])
        g_chosen = sb("g_chosen", [T, G])
        chosen = sb("chosen", [T, G, E])
        chosen_before = sb("chosen_before", [T, G, E])
        place = sb("place", [T, G, E])
        e_pick = sb("e_pick", [T, G, KE, E])
        e_work = sb("e_work", [T, G, KE, E])
        e_work2 = sb("e_work2", [T, G, KE, E])
        g_pick = sb("g_pick", [T, KG, G])
        g_work = sb("g_work", [T, KG, G, KE])
        g_work2 = sb("g_work2", [T, KG, G, KE])
        g_share_work = sb("g_share_work", [T, KG, G])
        pick_share = sb("pick_share", [T, KG, KE])
        e_place = sb("e_place", [T, G, KE])
        e_share = sb("e_share", [T, G, KE])
        g_share = sb("g_share", [T, KG])
        pick_place = sb("pick_place", [T, KG, KE])
        places = ctx.enter_context(nc.sbuf_tensor("places", [T, B, KG * KE], I32))
        entries = sb("entries", [T, B, KG * KE, 2])
        ranks8 = sb("ranks8", [T, E])
        region = sb("region", [T, NE])
        later = sb("later", [T, T])
        ones = sb("ones", [T, SLOTS])
        blank = sb("blank", [128, CHUNKS // 128, SLOTS, 2])
        zeros = sb("zeros", [128, D])
        limits = sb("limits", [128, NE, CPE])
        full = sb("full", [128, NE, CPE])
        e_tiles = sb("e_tiles", [128, NE])
        sums = [sb(f"sums{i}", [128, NE]) for i in range(2)]
        passed = sb("passed", [128, NE])
        passed_tiles = sb("passed_tiles", [128, NE])
        tile_no = sb("tile_no", [128, 1])
        tile_expert = sb("tile_expert", [128, 1])
        tile_first = sb("tile_first", [128, 1])
        tile_chunk = sb("tile_chunk", [128, 1])
        chunk_idx = ctx.enter_context(nc.sbuf_tensor("chunk_idx", [128, 1], I32))
        expert_row = ctx.enter_context(nc.sbuf_tensor("expert_row", [1, 128], I32))
        group_first = sb("group_first", [1, SPARE_GROUPS])
        group_used = sb("group_used", [1, SPARE_GROUPS])
        group_count = sb("group_count", [1, 1])
        groups_run = ctx.enter_context(nc.sbuf_tensor("groups_run", [1, 1], I32))
        listed = sb("listed", [128, SLOTS, 2])
        ident128 = sb("ident128", [128, 128])
        slot_token = ctx.enter_context(nc.sbuf_tensor("slot_token", [SLOTS, 128], I32))
        slot_gate = sb("slot_gate", [SLOTS, 128])
        w1_sb = [sb(f"w1_sb{i}", [HALF, 2, HID]) for i in range(2)]
        w2_sb = [sb(f"w2_sb{i}", [128, HC, D]) for i in range(2)]
        b1_sb = [sb(f"b1_sb{i}", [128, HC]) for i in range(2)]
        b2_sb = [sb(f"b2_sb{i}", [SLOTS, D]) for i in range(2)]
        x_rows = [sb(f"x_rows{i}", [SLOTS, D]) for i in range(X_BUFS)]
        x_T = [sb(f"x_T{i}", [HALF, 2, SLOTS]) for i in range(2)]
        hid = [sb(f"hid{i}", [128, HC, SLOTS]) for i in range(2)]
        y_rows = [sb(f"y_rows{i}", [SLOTS, D]) for i in range(2)]
        w1_in = [sem(f"w1_in{i}") for i in range(2)]
        w2_in = [sem(f"w2_in{i}") for i in range(2)]
        b1_in = [sem(f"b1_in{i}") for i in range(2)]
        b2_in = [sem(f"b2_in{i}") for i in range(2)]
        x_in = [sem(f"x_in{i}") for i in range(X_BUFS)]

        bank = [ctx.enter_context(nc.psum_tensor(f"bank{i}", [128, 512], F32)) for i in range(8)]

        patches_in = [sem(f"patches_in{g}") for g in range(GROUPS)]
        h_in = [sem(f"h_in{g}") for g in range(GROUPS)]

        names = """
        tok_loaded first_loaded loaded consts_set blank_out zeros_out tok_done tok_added h0_added
        stats_done meanvar_done vareps_done rstd_done xn_done xnT_done xnT_copied
        qk_done qk_copied v_done v_copied k_wide_done scores_done max_done shifted_done turned scores_exped
        pv_done o1_recip o1_done o1T_done o1T_copied proj1_done
        squared norm2_done normclamp_done norminv_done t_done tT_done tT_copied t_wide_done
        sim_done exp2_done mask2_done pv2_done o2_recip o2_done o2T_done o2T_copied proj2_done h2_done
        stats2_done meanvar2_done vareps2_done rstd2_done xf_done xfT_done xfT_copied rows_out base_out
        router_done logits_copied ranking below_done route_exped ranked pos_done place_done choosing
        choices_done scattered
        totals_done listing groups_ready chunk_ready tiles_listed expert_turned expert_ready
        list_in list_turned list_copied
        x_turned x_copied up_done hid_done down_done y_added y_done y_out finished""".split()
        S = {n: sem(n) for n in names}

        first_loads = [(qkv_w_sb, qkv_w), (ident, identity), (head_mask_sb, head_mask), (proj_w_sb, proj_w)]
        first_done = 16 * (len(first_loads) + 1)
        loads = [
            (router_w_sb, router_w), (earlier_sb, earlier),
            (later, later_c), (region, region_c), (ranks8, ranks8_c), (entries, entries_c),
            (limits, limits_c), (tile_no, tile_no_c), (ident128, ident128_c), (group_first, group_first_c),
            (blank, blank_c),
        ]
        loads_done = 16 * len(loads)

        def wait(eng, name, b):
            if isinstance(b, int) and b < 0:
                return
            eng.wait_ge(S[name], b + 1)

        def apart(eng):
            eng.wait_ge(S["consts_set"], CONSTANTS)

        def pipeline(eng, body):
            for i in range(4):
                body(i)
            with eng.Fori(4, B - 1) as i:
                body(i)
            for i in range(B - 1, B + 3):
                body(i)

        def stages(i):
            return tuple(i - k if not isinstance(i, int) or 0 <= i - k < B else None for k in range(4))

        def next_image(i):
            return i + 1 if not isinstance(i, int) or i + 1 < B else None

        def wait_half(eng, name, b, half):
            if isinstance(b, int) and b < 0:
                return
            eng.wait_ge(S[name], 2 * b + half + 1)

        def heads_of(half):
            return slice(half * HG, (half + 1) * HG)

        groups_at = {0: (3,), 1: (4,), 2: (5,)}
        embed_bank = [bank[6], bank[5], bank[4]] + [bank[6]] * (GROUPS - 3)

        def groups_needed(eng):
            eng.wait_ge(S["groups_ready"], 1)
            return eng.value_load(groups_run[0:1, 0:1], min_val=0, max_val=SPARE_GROUPS)

        def images_of(g):
            return range(g * GROUP, min(B, (g + 1) * GROUP))

        scores_bank = [bank[0], bank[1]]
        sim_bank = [bank[2], bank[3]]
        block = ctx.enter_context(nc.Block())

        @block.sync
        def _(sp):
            sp.dma_start(tok_w_sb[:], tok_w).then_inc(S["tok_loaded"], 16)
            sp.dma_start(patches_sb[:, 0], patches[0]).then_inc(patches_in[0], 16)
            sp.dma_start(tok_b_sb[:], tok_b).then_inc(S["tok_loaded"], 16)
            sp.dma_start(patches_sb[:, 1], patches[1]).then_inc(patches_in[1], 16)
            sp.dma_start(h_sb[PATCH_TOK:T, :, :], txt).then_inc(S["first_loaded"], 16)
            for dst, src in first_loads:
                sp.dma_start(dst[:], src).then_inc(S["first_loaded"], 16)

            def spread(g):
                wait(sp, "tok_added", g)
                for n, b in enumerate(images_of(g)):
                    if b == 0:
                        continue
                    sp.dma_start(h_sb[0:PATCH_TOK, b, :], embedded[n * PATCH_TOK:(n + 1) * PATCH_TOK, g, :]
                                 ).then_inc(h_in[g], 16)
            sp.dma_start(patches_sb[:, 2], patches[2]).then_inc(patches_in[2], 16)
            spread(0)
            for g in range(3, GROUPS):
                sp.dma_start(patches_sb[:, g], patches[g]).then_inc(patches_in[g], 16)
            spread(1)
            spread(2)
            for dst, src in loads:
                sp.dma_start(dst[:], src).then_inc(S["loaded"], 16)

            sp.wait_ge(S["loaded"], loads_done)
            sp.dma_start(table.rearrange("(p c) w -> p (c w)", p=128), blank[:].rearrange("p c s w -> p (c s w)")
                         ).then_inc(S["blank_out"], 16)
            sp.wait_ge(S["consts_set"], CONSTANTS)
            sp.dma_start(xf_rows[TOKENS:TOKENS + SLOTS, :], zeros[:]).then_inc(S["zeros_out"], 16)
            sp.dma_start(out[TOKENS:TOKENS + SLOTS, :], zeros[:]).then_inc(S["zeros_out"], 16)

            def turn(i):
                _, _, c, _ = stages(i)
                if isinstance(i, int):
                    for g in groups_at.get(i, ()):
                        spread(g)
                if c is not None:
                    wait(sp, "xf_done", c)
                    sp.dma_start(xf_rows[bass.ds(c * T, T), :], xf[:]).then_inc(S["rows_out"], 16)
                    wait(sp, "h2_done", c)
                    sp.dma_start(out[bass.ds(c * T, T), :], h_sb[:, c, :]).then_inc(S["base_out"], 16)

            pipeline(sp, turn)


            def expert_of(i):
                return sp.value_load(expert_row[0:1, bass.ds(i, 1)], min_val=0, max_val=NE - 1)

            def load_w1(e, p):
                sp.dma_start(w1_sb[p][:], w1[e]).then_inc(w1_in[p], 16)

            def load_b1(e, p):
                sp.dma_start(b1_sb[p][:], b1[e]).then_inc(b1_in[p], 16)

            def load_rest(e, p):
                sp.dma_start(w2_sb[p][:], w2[e]).then_inc(w2_in[p], 16)
                sp.dma_start(b2_sb[p][:], b2[bass.ds(e, 1), :].to_broadcast([SLOTS, D])).then_inc(b2_in[p], 16)

            def renew_w1(i, p):
                e = expert_of(i)
                before = expert_of(i - 2)
                with sp.If(e != before):
                    sp.wait_ge(S["up_done"], HC * (i - 1))
                    load_w1(e, p)
                    sp.wait_ge(S["hid_done"], HC * (i - 1))
                    load_b1(e, p)
                with sp.Else():
                    sp.wait_ge(S["up_done"], HC * (i - 1))
                    sp.sem_inc(w1_in[p], 16)
                    sp.wait_ge(S["hid_done"], HC * (i - 1))
                    sp.sem_inc(b1_in[p], 16)

            def renew_rest(i, p):
                def free():
                    sp.wait_ge(S["down_done"], i - 1)
                    sp.wait_ge(S["y_added"], i - 1)
                e = expert_of(i)
                before = expert_of(i - 2)
                with sp.If(e != before):
                    free()
                    load_rest(e, p)
                with sp.Else():
                    free()
                    for s in (w2_in, b2_in):
                        sp.sem_inc(s[p], 16)

            sp.wait_ge(S["expert_ready"], 1)
            for i in range(2):
                e = expert_of(i)
                load_w1(e, i)
                load_b1(e, i)
                load_rest(e, i)
            renew_w1(2, 0)
            renew_w1(3, 1)
            renew_rest(2, 0)

            def two(q):
                for p in range(2):
                    renew_w1(2 * q + p, p)
                    renew_rest(2 * q + p - 1, (p + 1) % 2)
            with sp.Fori(2, SURE // 2) as q:
                two(q)
            groups = groups_needed(sp)
            n = X_BUFS * groups + SURE
            with sp.Fori(SURE // 2, TILES // 2) as q:
                with sp.If(2 * q < n):
                    two(q)
            renew_rest(X_BUFS * groups + SURE - 1, 1)
            sp.wait_ge(S["y_out"], 16 * n)
            sp.sem_inc(S["finished"], 1)
            sp.wait_ge(S["finished"], 1)

        @block.gpsimd
        def _(pool):
            constants = ([(minus_half[:], -0.5), (eps[:], LN_EPS)]
                         + [(buf[HALF:HALF + 1, :, :], 1.0) for buf in (xn_T, o1_T, o2_T, xf_cur)]
                         + [(v_sb[:, :, :, HD:HD + 1], 1.0), (ones[:], 1.0), (chosen[:], 0.0),
                            (chosen_before[:], 0.0), (zeros[:], 0.0)])
            for n, (dst, value) in enumerate(constants):
                if n > 0:
                    pool.wait_ge(S["consts_set"], n)
                pool.memset(dst, value).then_inc(S["consts_set"], 1)
            pool.wait_ge(S["consts_set"], CONSTANTS)
            pool.wait_ge(S["first_loaded"], first_done)

            def inverse_root(mv, tmp, dst, done1, done2, b):
                pool.tensor_tensor(tmp[:], mv[:, 1:2], eps[:], ALU.add).then_inc(S[done1], 1)
                wait(pool, done1, b)
                pool.tensor_tensor(dst[:], tmp[:], minus_half[:, 0:1], ALU.pow).then_inc(S[done2], 1)

            def scatter(b, choices):
                for j in choices:
                    pool.indirect_dma_start(
                        out=table, out_offset=bass.IndirectOffsetOnAxis(ap=places[:, b, j:j + 1], axis=0),
                        in_=entries[:, b, j, :], in_offset=None).then_inc(S["scattered"], 16)

            def turn(i):
                a, b, c, d = stages(i)
                if i >= 4:
                    scatter(i - 4, range(KG * KE - 1, KG * KE))
                if b is not None:
                    wait(pool, "norm2_done", b)
                    wait(pool, "t_done", b - 1)
                    pool.tensor_scalar(norm2_clamped[:], norm2[:], NORM_EPS ** 2, None,
                                       ALU.max).then_inc(S["normclamp_done"], 1)
                    wait(pool, "normclamp_done", b)
                    pool.tensor_tensor(norm_inv[:], norm2_clamped[:], minus_half[:],
                                       ALU.pow).then_inc(S["norminv_done"], 1)
                if a is not None:
                    wait(pool, "qk_copied", a)
                    for half in range(2):
                        wait_half(pool, "scores_done", a - 1, half)
                        pool.tensor_tensor(
                            k_wide[:, half, :, :], qk_T[:, 2 + half, :].unsqueeze(1).to_broadcast([HALF, HG, T]),
                            head_mask_sb[:, :].unsqueeze(2).to_broadcast([HALF, HG, T]),
                            ALU.mult).then_inc(S["k_wide_done"], 1)
                if c is not None:
                    wait(pool, "meanvar2_done", c)
                    inverse_root(mean_var2, var_eps2, rstd2, "vareps2_done", "rstd2_done", c)
                if d is not None:
                    wait(pool, "choices_done", d)
                    if d == 0:
                        pool.wait_ge(S["loaded"], loads_done)
                        pool.wait_ge(S["blank_out"], 16)
                    scatter(d, range(KG * KE - 1))
                next_root(next_image(i))

            def next_root(b):
                if b is not None:
                    wait(pool, "meanvar_done", b)
                    inverse_root(mean_var, var_eps, rstd, "vareps_done", "rstd_done", b)

            next_root(0)
            for i in range(B + 4):
                turn(i)

            pool.wait_ge(S["scattered"], 16 * B * KG * KE)
            pool.wait_ge(S["chunk_ready"], 1)
            pool.indirect_dma_start(
                out=listed[:].rearrange("p s w -> p (s w)"), out_offset=None,
                in_=table.rearrange("(c s) w -> c (s w)", s=SLOTS),
                in_offset=bass.IndirectOffsetOnAxis(ap=chunk_idx[:], axis=0)).then_inc(S["list_in"], 16)

            pool.wait_ge(S["rows_out"], 16 * B)
            pool.wait_ge(S["base_out"], 16 * B)
            pool.wait_ge(S["zeros_out"], 32)
            pool.wait_ge(S["list_copied"], 1)

            def gather(i):
                if i >= X_BUFS:
                    pool.wait_ge(S["x_turned"], i - X_BUFS + 1)
                pool.indirect_dma_start(
                    out=x_rows[i % X_BUFS][:], out_offset=None, in_=xf_rows,
                    in_offset=bass.IndirectOffsetOnAxis(ap=slot_token[:, i:i + 1], axis=0)
                ).then_inc(x_in[i % X_BUFS], 16)

            for i in range(X_BUFS + 1):
                gather(i)

            def tile(i):
                pool.wait_ge(S["y_done"], i + 1)
                if i >= 1:
                    pool.wait_ge(S["y_out"], 16 * i)
                pool.indirect_dma_start(
                    out=out, out_offset=bass.IndirectOffsetOnAxis(ap=slot_token[:, i:i + 1], axis=0),
                    in_=y_rows[i % 2][:], in_offset=None, compute_op=ALU.add).then_inc(S["y_out"], 16)
                if i + X_BUFS + 1 <= TILES:
                    gather(i + X_BUFS + 1)

            for i in range(SURE):
                tile(i)
            groups = groups_needed(pool)
            n = X_BUFS * groups + SURE
            for first in range(SURE, TILES, X_BUFS):
                with pool.If(n > first):
                    for i in range(first, first + X_BUFS):
                        tile(i)

        @block.scalar
        def _(act):
            act.wait_ge(S["consts_set"], CONSTANTS)

            def copy_halves(dst, psum, done):
                act.activation(dst, psum[0:HALF, 0:2 * T].rearrange("p (g t) -> p g t", g=2),
                               ACT.Copy).then_inc(S[done], 1)

            def exp_half(dst, psum, half, scale, done):
                act.activation(dst[:, heads_of(half), :].rearrange("p h t -> p (h t)"),
                               psum[half][0:T, 0:HG * T], ACT.Exp, scale=scale).then_inc(S[done], 1)

            def turn(i):
                a, b, c, d = stages(i)
                if a is not None:
                    wait(act, "xnT_done", a)
                    wait(act, "v_done", a - 1)
                    copy_halves(xn_T[0:HALF, :, :], bank[7], "xnT_copied")
                if b is not None:
                    wait(act, "proj1_done", b)
                    wait(act, "norm2_done", b - 1)
                    act.activation(squares[:].rearrange("p h d -> p (h d)"), bank[4][0:T, 0:D],
                                   ACT.Square).then_inc(S["squared"], 1)
                if c is not None:
                    wait(act, "o2T_done", c)
                    wait(act, "proj2_done", c - 1)
                    copy_halves(o2_T[0:HALF, :, :], bank[7], "o2T_copied")
                if a is not None:
                    wait(act, "qk_done", a)
                    wait_half(act, "k_wide_done", a - 1, 1)
                    wait_half(act, "scores_done", a - 1, 1)
                    act.activation(qk_T[:].rearrange("p q t -> p (q t)"), bank[5][0:HALF, 0:4 * T],
                                   ACT.Copy).then_inc(S["qk_copied"], 1)
                if b is not None:
                    wait(act, "tT_done", b)
                    wait_half(act, "sim_done", b - 1, 1)
                    copy_halves(t_T[:], bank[4], "tT_copied")
                    for half in range(2):
                        for h in range(HG):
                            ins = act.activation(t_wide[:, half, h, :], bank[4][0:HALF, half * T:(half + 1) * T],
                                                 ACT.Copy, scale=head_mask_sb[:, h:h + 1])
                        ins.then_inc(S["t_wide_done"], 1)
                if a is not None:
                    apart(act)
                    wait(act, "v_done", a)
                    act.activation(v_sb[:, a, :, 0:HD],
                                   bank[7][0:T, 0:D].rearrange("p (h d) -> p h d", h=HEADS),
                                   ACT.Copy).then_inc(S["v_copied"], 1)
                if b is not None:
                    wait_half(act, "sim_done", b, 0)
                    wait_half(act, "mask2_done", b - 1, 0)
                    exp_half(sim_exp, sim_bank, 0, SIM_SCALE, "exp2_done")
                if c is not None:
                    wait(act, "xfT_done", c)
                    wait(act, "router_done", c - 1)
                    copy_halves(xf_cur[0:HALF, :, :], bank[5], "xfT_copied")
                if b is not None:
                    wait_half(act, "sim_done", b, 1)
                    wait_half(act, "mask2_done", b - 1, 1)
                    exp_half(sim_exp, sim_bank, 1, SIM_SCALE, "exp2_done")
                if c is not None:
                    wait(act, "router_done", c)
                    wait(act, "ranked", c - 1)
                    act.activation(logits[:], bank[6][0:T, 0:R], ACT.Copy).then_inc(S["logits_copied"], 1)
                if a is not None:
                    for half in range(2):
                        wait_half(act, "turned", a, half)
                        wait_half(act, "pv_done", a - 1, half)
                        exp_half(probs_T, scores_bank, half, ATT_SCALE, "scores_exped")
                if c is not None:
                    wait(act, "below_done", c)
                    wait(act, "choices_done", c - 1)
                    act.activation(exps[:], below[:], ACT.Exp).then_inc(S["route_exped"], 1)
                if a is not None:
                    wait(act, "o1T_done", a)
                    wait(act, "proj1_done", a - 1)
                    copy_halves(o1_T[0:HALF, :, :], bank[7], "o1T_copied")

            pipeline(act, turn)

            def tile(i, p, turns):
                act.wait_ge(b1_in[p], 16 * turns)
                if not (isinstance(i, int) and i < 2):
                    act.wait_ge(S["down_done"], i - 1)
                for c in range(HC):
                    act.wait_ge(S["up_done"], HC * i + c + 1)
                    act.activation(hid[p][:, c, :], bank[(HC * p + c) % 4][:, 0:SLOTS], ACT.Gelu,
                                   bias=b1_sb[p][:, c:c + 1]).then_inc(S["hid_done"], 1)

            for i in range(2):
                tile(i, i, 1)
            with act.Fori(1, SURE // 2) as q:
                for p in range(2):
                    tile(2 * q + p, p, q + 1)
            groups = groups_needed(act)
            n = X_BUFS * groups + SURE
            with act.Fori(SURE // 2, TILES // 2) as q:
                with act.If(2 * q < n):
                    for p in range(2):
                        tile(2 * q + p, p, q + 1)

        @block.tensor
        def _(pe):
            def embed(g):
                pe.wait_ge(S["tok_loaded"], 32)
                pe.wait_ge(patches_in[g], 16)
                if g >= 3:
                    wait(pe, "tok_added", g - 1)
                rows = len(images_of(g)) * PATCH_TOK
                for k in range(PK):
                    ins = pe.matmul(embed_bank[g][0:rows, 0:D], patches_sb[:, g, k, 0:rows], tok_w_sb[:, k, :],
                                    start=(k == 0), stop=(k == PK - 1))
                ins.then_inc(S["tok_done"], 1)
            for g in range(3):
                embed(g)
            pe.wait_ge(S["first_loaded"], first_done)
            pe.wait_ge(S["consts_set"], CONSTANTS)

            def turn_halves(psum, src, done):
                for g in range(2):
                    ins = pe.transpose(psum[0:HALF, g * T:(g + 1) * T], src[:, g * HALF:(g + 1) * HALF], ident[:])
                ins.then_inc(S[done], 1)

            def linear(psum, x_T, w, done):
                for g in range(2):
                    k = HALF + g
                    ins = pe.matmul(psum, x_T[0:k, g], w[0:k, g, :], start=(g == 0), stop=(g == 1))
                ins.then_inc(S[done], 1)

            def weighted_values(psum, weights, b, half, done):
                for h in range(half * HG, (half + 1) * HG):
                    ins = pe.matmul(psum[0:T, h * (HD + 1):(h + 1) * (HD + 1)], weights[:, h, :],
                                    v_sb[:, b, h, :], start=True, stop=True)
                ins.then_inc(S[done], 1)

            def pairs(psum, rows_T, wide, half, done):
                pe.matmul(psum[half][0:T, 0:HG * T], rows_T, wide[:, half, :, :].rearrange("p h t -> p (h t)"),
                          start=True, stop=True).then_inc(S[done], 1)

            def turn(i):
                a, b, c, d = stages(i)
                if b is not None:
                    wait(pe, "o1T_copied", b)
                if a is not None:
                    wait(pe, "xn_done", a)
                    turn_halves(bank[7], xn, "xnT_done")
                if b is not None:
                    linear(bank[4][0:T, 0:D], o1_T, proj_w_sb, "proj1_done")
                if c is not None:
                    wait(pe, "o2_done", c)
                    if a is not None:
                        wait(pe, "xnT_copied", a)
                    turn_halves(bank[7], o2, "o2T_done")
                if d is not None:
                    wait(pe, "ranked", d)
                    pe.matmul(bank[6][0:T, 0:NE], later[:], chosen[:].rearrange("p g e -> p (g e)"),
                              start=True, stop=False)
                    pe.matmul(bank[6][0:T, 0:NE], ones[:, 0:T], chosen_before[:].rearrange("p g e -> p (g e)"),
                              start=False, stop=True).then_inc(S["pos_done"], 1)
                if a is not None:
                    wait(pe, "xnT_copied", a)
                    if isinstance(i, int) and i == 0:
                        wait(pe, "tok_added", 2)
                    for q in range(4):
                        for g in range(2):
                            k = HALF + g
                            ins = pe.matmul(bank[5][0:HALF, q * T:(q + 1) * T],
                                            qkv_w_sb[0:k, g, q * HALF:(q + 1) * HALF], xn_T[0:k, g, :],
                                            start=(g == 0), stop=(g == 1))
                    ins.then_inc(S["qk_done"], 1)
                if c is not None:
                    wait(pe, "o2T_copied", c)
                    if d is not None:
                        wait(pe, "place_done", d)
                    if isinstance(i, int) and i - 1 in groups_at:
                        wait(pe, "tok_added", groups_at[i - 1][-1])
                    linear(bank[6][0:T, 0:D], o2_T, proj_w_sb, "proj2_done")
                if b is not None:
                    wait(pe, "t_done", b)
                    turn_halves(bank[4], t_tok, "tT_done")
                if a is not None:
                    linear(bank[7][0:T, 0:D], xn_T, qkv_w_sb[:, :, 2 * D:3 * D], "v_done")
                if a is not None:
                    wait(pe, "qk_copied", a)
                    for half in range(2):
                        wait_half(pe, "k_wide_done", a, half)
                        pairs(scores_bank, qk_T[:, half, :], k_wide, half, "scores_done")
                if b is not None:
                    wait(pe, "tT_copied", b)
                    wait_half(pe, "t_wide_done", b, 0)
                    pairs(sim_bank, t_T[:, 0, :], t_wide, 0, "sim_done")
                if c is not None:
                    wait(pe, "xf_done", c)
                    turn_halves(bank[5], xf, "xfT_done")
                if b is not None:
                    wait_half(pe, "t_wide_done", b, 1)
                    pairs(sim_bank, t_T[:, 1, :], t_wide, 1, "sim_done")
                if c is not None:
                    if isinstance(i, int) and c == 0:
                        pe.wait_ge(S["loaded"], loads_done)
                    wait(pe, "xfT_copied", c)
                    linear(bank[6][0:T, 0:R], xf_cur, router_w_sb, "router_done")
                if a is not None:
                    for half in range(2):
                        wait_half(pe, "shifted_done", a, half)
                        for h in range(half * HG, (half + 1) * HG):
                            ins = pe.transpose(scores_bank[half][0:T, h % HG * T:(h % HG + 1) * T],
                                               shifted[:, h, :], ident[:])
                        ins.then_inc(S["turned"], 1)
                    wait(pe, "v_copied", a)
                    for half in range(2):
                        wait_half(pe, "scores_exped", a, half)
                        weighted_values(bank[4], probs_T, a, half, "pv_done")
                if b is not None:
                    wait_half(pe, "mask2_done", b, 0)
                    weighted_values(bank[5], sim_probs, b, 0, "pv2_done")
                if a is not None:
                    wait(pe, "o1_done", a)
                    turn_halves(bank[7], o1, "o1T_done")
                if b is not None:
                    wait_half(pe, "mask2_done", b, 1)
                    weighted_values(bank[5], sim_probs, b, 1, "pv2_done")
                if isinstance(i, int):
                    for g in groups_at.get(i, ()):
                        embed(g)

            pipeline(pe, turn)

            wait(pe, "ranked", B - 1)
            wait(pe, "place_done", B - 1)
            pe.matmul(bank[6][:, 0:NE], ones[:], chosen[:].rearrange("p g e -> p (g e)"), start=True, stop=False)
            pe.matmul(bank[6][:, 0:NE], ones[:], chosen_before[:].rearrange("p g e -> p (g e)"), start=False,
                      stop=True).then_inc(S["totals_done"], 1)
            pe.wait_ge(S["tiles_listed"], 1)
            pe.transpose(bank[5][0:1, 0:128], tile_expert[:], ident128[:]).then_inc(S["expert_turned"], 1)
            pe.wait_ge(S["list_in"], 16)
            for w in range(2):
                pe.transpose(bank[w][0:SLOTS, 0:128], listed[:, :, w], ident128[:]).then_inc(S["list_turned"], 1)
            pe.wait_ge(S["list_copied"], 2)

            def turn_x(i, r):
                pe.wait_ge(x_in[r[0]], 16 * r[1])
                if not (isinstance(i, int) and i < 2):
                    pe.wait_ge(S["x_copied"], i - 1)
                for g in range(2):
                    ins = pe.transpose(bank[6 + r[0] % 2][0:HALF, g * SLOTS:(g + 1) * SLOTS],
                                       x_rows[r[0]][:, g * HALF:(g + 1) * HALF], ident128[:])
                ins.then_inc(S["x_turned"], 1)

            def up(i, p, turns):
                pe.wait_ge(S["x_copied"], i + 1)
                pe.wait_ge(w1_in[p], 16 * turns)
                for c in range(HC):
                    if not (isinstance(i, int) and HC * i + c < 4):
                        pe.wait_ge(S["hid_done"], HC * i + c - 3)
                    for g in range(2):
                        ins = pe.matmul(bank[(HC * p + c) % 4][:, 0:SLOTS], w1_sb[p][:, g, c * 128:(c + 1) * 128],
                                        x_T[p][:, g, :], start=(g == 0), stop=(g == 1))
                    ins.then_inc(S["up_done"], 1)

            def down(i, p, turns):
                pe.wait_ge(S["hid_done"], HC * (i + 1))
                pe.wait_ge(w2_in[p], 16 * turns)
                if not (isinstance(i, int) and i < 2):
                    pe.wait_ge(S["y_added"], i - 1)
                for c in range(HC):
                    ins = pe.matmul(bank[4 + p][0:SLOTS, 0:D], hid[p][:, c, :], w2_sb[p][:, c, :],
                                    start=(c == 0), stop=(c == HC - 1))
                ins.then_inc(S["down_done"], 1)

            turn_x(0, (0, 1))
            def four(q, first=False):
                for r in range(4):
                    i = 4 * q + r
                    turn_x(i + 1, ((r + 1) % 4, q + 1 + (r == 3)))
                    up(i, r % 2, 2 * q + r // 2 + 1)
                    if not (first and r == 0):
                        down(i - 1, (r + 1) % 2, 2 * q + (r + 1) // 2)
            four(0, first=True)
            with pe.Fori(1, SURE // 4) as q:
                four(q)
            groups = groups_needed(pe)
            n = X_BUFS * groups + SURE
            with pe.Fori(SURE // 4, TILES // 4) as q:
                with pe.If(4 * q < n):
                    four(q)
            down(X_BUFS * groups + SURE - 1, 1, 2 * groups + SURE // 2)

        @block.vector
        def _(dve):
            def add_bias(g):
                rows = len(images_of(g)) * PATCH_TOK
                wait(dve, "tok_done", g)
                dve.tensor_tensor(embedded[0:rows, g, :], embed_bank[g][0:rows, 0:D], tok_b_sb[0:rows, :],
                                  ALU.add).then_inc(S["tok_added"], 1)
            dve.wait_ge(S["tok_loaded"], 32)
            wait(dve, "tok_done", 0)
            dve.tensor_tensor(h_sb[0:PATCH_TOK, 0, :], embed_bank[0][0:PATCH_TOK, 0:D], tok_b_sb[0:PATCH_TOK, :],
                              ALU.add).then_inc(S["h0_added"], 1)
            add_bias(0)
            dve.wait_ge(S["first_loaded"], first_done)
            dve.wait_ge(S["consts_set"], CONSTANTS)

            def by_head(psum):
                return psum[0:T, 0:HEADS * (HD + 1)].rearrange("p (h d) -> p h d", h=HEADS)

            def normalise(psum, inv, dst, free, recip, done, b):
                pv = by_head(psum)
                wait(dve, done, b - 1)
                dve.reciprocal(inv[:].unsqueeze(2), pv[:, :, HD:HD + 1]).then_inc(S[recip], 1)
                wait(dve, recip, b)
                wait(dve, free, b - 1)
                dve.tensor_tensor(dst[:].rearrange("p (h d) -> p h d", h=HEADS), pv[:, :, 0:HD],
                                  inv[:].unsqueeze(2).to_broadcast([T, HEADS, HD]), ALU.mult).then_inc(S[done], 1)

            def moments(src, st, mv, h_ready, st_done, free, done, b):
                apart(dve)
                wait(dve, h_ready, b)
                wait(dve, done, b - 1)
                dve.bn_stats(st[:], src).then_inc(S[st_done], 1)
                apart(dve)
                wait(dve, st_done, b)
                wait(dve, free, b - 1)
                dve.bn_aggr(mv[:], st[:]).then_inc(S[done], 1)

            def chain(b, total, name, before=0):
                n = [before]

                def then(ins):
                    n[0] += 1
                    ins.then_inc(S[name], 1)
                    dve.wait_ge(S[name], total * b + n[0])
                return then

            e_flat = "p g e -> p (g e)"

            def tops_of(r):
                then = chain(r, 6, "ranking")
                if isinstance(r, int) and r == 0:
                    dve.wait_ge(S["loaded"], loads_done)
                wait(dve, "logits_copied", r)
                e_logits = logits[:, G:R].rearrange("p (g e) -> p g e", g=G)
                four, three = [T, G, E, E], [T, G, G]
                ei, ej = e_logits.unsqueeze(3).to_broadcast(four), e_logits.unsqueeze(2).to_broadcast(four)
                gi = logits[:, 0:G].unsqueeze(2).to_broadcast(three)
                gj = logits[:, 0:G].unsqueeze(1).to_broadcast(three)
                dve.tensor_reduce(tops[:, 0:G], e_logits, AX.X, ALU.max)
                dve.tensor_reduce(tops[:, G:G + 1], logits[:, 0:G], AX.X, ALU.max)
                dve.tensor_tensor(g_ties[:], gj, gi, ALU.is_equal)
                then(dve.tensor_tensor(ties[:], ej, ei, ALU.is_equal))
                wait(dve, "route_exped", r - 1)
                dve.tensor_tensor(below[:, G:R].rearrange("p (g e) -> p g e", g=G), e_logits,
                                  tops[:, 0:G].unsqueeze(2).to_broadcast([T, G, E]), ALU.subtract)
                dve.tensor_scalar(below[:, 0:G], logits[:, 0:G], tops[:, G:G + 1], None,
                                  ALU.subtract).then_inc(S["below_done"], 1)
                dve.tensor_tensor(g_ties[:], g_ties[:], earlier_sb[:, 0:G, 0:G], ALU.mult)
                dve.tensor_tensor(ties[:], ties[:], earlier_sb[:].unsqueeze(1).to_broadcast(four), ALU.mult)
                dve.tensor_tensor(g_beats[:], gj, gi, ALU.is_gt)
                then(dve.tensor_tensor(beats[:], ej, ei, ALU.is_gt))

            def ranks(r):
                then = chain(r, 6, "ranking", 2)
                four = [T, G, E, E]
                dve.tensor_tensor(g_beats[:], g_beats[:], g_ties[:], ALU.add)
                then(dve.tensor_tensor(beats[:], beats[:], ties[:], ALU.add))
                dve.tensor_reduce(g_rank[:], g_beats[:], AX.X, ALU.add)
                then(dve.tensor_reduce(e_rank[:], beats[:], AX.X, ALU.add))

            def choose(r):
                then = chain(r, 6, "ranking", 4)
                wait(dve, "pos_done", r - 1)
                then(dve.tensor_tensor(chosen_before[:], chosen_before[:], chosen[:], ALU.add))
                dve.tensor_scalar(g_chosen[:], g_rank[:], float(KG), None, ALU.is_lt)
                then(dve.tensor_scalar(chosen[:].rearrange(e_flat), e_rank[:].rearrange(e_flat), float(KE), None,
                                       ALU.is_lt))
                dve.tensor_tensor(chosen[:], chosen[:], g_chosen[:].unsqueeze(2).to_broadcast([T, G, E]),
                                  ALU.mult).then_inc(S["ranked"], 1)

            wide = [T, G, KE, E]
            mid = [T, KG, G, KE]

            def picks(r):
                then = chain(r, 9, "choosing")
                wait(dve, "route_exped", r)
                dve.scalar_tensor_tensor(g_gate[:], g_rank[:], float(KG), exps[:, 0:G], ALU.is_lt, ALU.mult)
                dve.scalar_tensor_tensor(e_gate[:].rearrange(e_flat), e_rank[:].rearrange(e_flat), float(KE),
                                         exps[:, G:R], ALU.is_lt, ALU.mult)
                dve.tensor_tensor(g_pick[:], g_rank[:].unsqueeze(1).to_broadcast([T, KG, G]),
                                  ranks8[:, 0:KG].unsqueeze(2).to_broadcast([T, KG, G]), ALU.is_equal)
                then(dve.tensor_tensor(e_pick[:], e_rank[:].unsqueeze(2).to_broadcast(wide),
                                       ranks8[:, 0:KE].unsqueeze(1).unsqueeze(3).to_broadcast(wide), ALU.is_equal))
                dve.tensor_reduce(gate_sum[:, 0:G], e_gate[:], AX.X, ALU.add)
                dve.tensor_reduce(gate_sum[:, G:G + 1], g_gate[:], AX.X, ALU.add)
                wait(dve, "place_done", r)
                then(dve.tensor_tensor(e_work[:], e_pick[:], place[:].unsqueeze(2).to_broadcast(wide), ALU.mult))

            def gates(r):
                then = chain(r, 9, "choosing", 2)
                dve.reciprocal(gate_inv[:], gate_sum[:])
                then(dve.tensor_reduce(e_place[:], e_work[:], AX.X, ALU.add))
                dve.tensor_scalar(g_gate[:], g_gate[:], gate_inv[:, G:G + 1], None, ALU.mult)
                dve.tensor_tensor(e_gate[:], e_gate[:], gate_inv[:, 0:G].unsqueeze(2).to_broadcast([T, G, E]),
                                  ALU.mult)
                then(dve.tensor_tensor(g_work[:], g_pick[:].unsqueeze(3).to_broadcast(mid),
                                       e_place[:].unsqueeze(1).to_broadcast(mid), ALU.mult))
                dve.scalar_tensor_tensor(g_gate[:], g_gate[:], GATE_EPS, g_gate[:], ALU.is_ge, ALU.mult)
                dve.scalar_tensor_tensor(e_gate[:].rearrange(e_flat), e_gate[:].rearrange(e_flat), GATE_EPS,
                                         e_gate[:].rearrange(e_flat), ALU.is_ge, ALU.mult)
                then(dve.tensor_reduce(pick_place[:], g_work[:].rearrange("p r g k -> p r k g"), AX.X, ALU.add))

            def choices(r):
                then = chain(r, 9, "choosing", 5)
                dve.tensor_tensor(g_share_work[:], g_pick[:], g_gate[:].unsqueeze(1).to_broadcast([T, KG, G]),
                                  ALU.mult)
                dve.tensor_tensor(e_work2[:], e_pick[:], e_gate[:].unsqueeze(2).to_broadcast(wide), ALU.mult)
                then(dve.tensor_scalar(places[:, r, :], pick_place[:].rearrange("p r k -> p (r k)"), 0.0, None,
                                       ALU.add))
                dve.tensor_reduce(g_share[:], g_share_work[:], AX.X, ALU.add)
                then(dve.tensor_reduce(e_share[:], e_work2[:], AX.X, ALU.add))
                then(dve.tensor_tensor(g_work2[:], g_pick[:].unsqueeze(3).to_broadcast(mid),
                                       e_share[:].unsqueeze(1).to_broadcast(mid), ALU.mult))
                then(dve.tensor_reduce(pick_share[:], g_work2[:].rearrange("p r g k -> p r k g"), AX.X, ALU.add))
                dve.tensor_tensor(entries[:, r, :, 1].rearrange("p (r k) -> p r k", r=KG), pick_share[:],
                                  g_share[:].unsqueeze(2).to_broadcast([T, KG, KE]),
                                  ALU.mult).then_inc(S["choices_done"], 1)

            def layer_norm_stats(b):
                apart(dve)
                wait(dve, "meanvar_done", b - 1)
                dve.bn_stats(stats[:], h_sb[:, b, :]).then_inc(S["stats_done"], 1)
                wait(dve, "stats_done", b)
                wait(dve, "xn_done", b - 1)

            def layer_norm_moments():
                dve.bn_aggr(mean_var[:], stats[:]).then_inc(S["meanvar_done"], 1)

            def layer_norm(b):
                wait(dve, "rstd_done", b)
                wait(dve, "xnT_done", b - 1)
                dve.tensor_scalar(xn[:], h_sb[:, b, :], mean_var[:, 0:1], rstd[:], ALU.subtract,
                                  ALU.mult).then_inc(S["xn_done"], 1)

            def turn(i):
                a, b, c, d = stages(i)
                following = next_image(i)
                if c is not None:
                    wait_half(dve, "pv2_done", c, 1)
                    normalise(bank[5], sum2_inv, o2, "o2T_done", "o2_recip", "o2_done", c)
                if d is not None:
                    choose(d)
                if b is not None:
                    wait(dve, "squared", b)
                    wait(dve, "normclamp_done", b - 1)
                    dve.tensor_reduce(norm2[:], squares[:], AX.X, ALU.add).then_inc(S["norm2_done"], 1)
                if d is not None:
                    wait(dve, "pos_done", d)
                    dve.tensor_tensor(place[:].rearrange("p g e -> p (g e)"), bank[6][0:T, 0:NE], region[:],
                                      ALU.add).then_inc(S["place_done"], 1)
                    picks(d)
                    gates(d)
                if b is not None:
                    wait(dve, "norminv_done", b)
                    wait(dve, "tT_done", b - 1)
                    dve.tensor_tensor(t_tok[:].rearrange("p (h d) -> p h d", h=HEADS),
                                      bank[4][0:T, 0:D].rearrange("p (h d) -> p h d", h=HEADS),
                                      norm_inv[:].unsqueeze(2).to_broadcast([T, HEADS, HD]),
                                      ALU.mult).then_inc(S["t_done"], 1)
                if c is not None:
                    wait(dve, "proj2_done", c)
                    dve.tensor_tensor(h_sb[:, c, :], bank[6][0:T, 0:D], h_sb[:, c, :],
                                      ALU.add).then_inc(S["h2_done"], 1)
                    moments(h_sb[:, c, :], stats2, mean_var2, "h2_done", "stats2_done", "xf_done",
                            "meanvar2_done", c)
                if d is not None:
                    choices(d)
                if c is not None:
                    wait(dve, "rstd2_done", c)
                    if not (isinstance(c, int) and c == 0):
                        dve.wait_ge(S["rows_out"], 16 * c)
                    dve.tensor_scalar(xf[:], h_sb[:, c, :], mean_var2[:, 0:1], rstd2[:], ALU.subtract,
                                      ALU.mult).then_inc(S["xf_done"], 1)
                if a is not None:
                    for half in range(2):
                        scores = scores_bank[half][0:T, 0:HG * T].rearrange("p (h t) -> p h t", h=HG)
                        wait_half(dve, "scores_done", a, half)
                        wait_half(dve, "shifted_done", a - 1, half)
                        dve.tensor_reduce(row_max[:, heads_of(half)], scores, AX.X, ALU.max
                                          ).then_inc(S["max_done"], 1)
                    for half in range(2):
                        scores = scores_bank[half][0:T, 0:HG * T].rearrange("p (h t) -> p h t", h=HG)
                        wait_half(dve, "max_done", a, half)
                        wait_half(dve, "turned", a - 1, half)
                        dve.tensor_tensor(shifted[:, heads_of(half), :], scores,
                                          row_max[:, heads_of(half)].unsqueeze(2).to_broadcast([T, HG, T]),
                                          ALU.subtract).then_inc(S["shifted_done"], 1)
                if following is not None:
                    first_use = {0: (0,), 2: (1,), 3: range(2, GROUPS)}
                    for g in first_use.get(i, ()) if isinstance(i, int) else ():
                        dve.wait_ge(h_in[g], 16 * (len(images_of(g)) - (g == 0)))
                    layer_norm_stats(following)
                if b is not None:
                    for half in range(2):
                        wait_half(dve, "exp2_done", b, half)
                        wait_half(dve, "pv2_done", b - 1, half)
                        dve.scalar_tensor_tensor(
                            sim_probs[:, heads_of(half), :].rearrange("p h t -> p (h t)"),
                            sim_bank[half][0:T, 0:HG * T], 0.0,
                            sim_exp[:, heads_of(half), :].rearrange("p h t -> p (h t)"), ALU.is_ge, ALU.mult
                        ).then_inc(S["mask2_done"], 1)
                if following is not None:
                    layer_norm_moments()
                if c is not None:
                    tops_of(c)
                if a is not None:
                    wait_half(dve, "pv_done", a, 1)
                    normalise(bank[4], sum_inv, o1, "o1T_done", "o1_recip", "o1_done", a)
                if following is not None:
                    layer_norm(following)
                if c is not None:
                    ranks(c)
                if isinstance(i, int):
                    for g in groups_at.get(i, ()):
                        add_bias(g)

            dve.wait_ge(S["h0_added"], 1)
            layer_norm_stats(0)
            add_bias(1)
            layer_norm_moments()
            layer_norm(0)
            add_bias(2)
            pipeline(dve, turn)
            count = [0]

            def then(ins):
                count[0] += 1
                ins.then_inc(S["listing"], 1)
                dve.wait_ge(S["listing"], count[0])

            dve.wait_ge(S["totals_done"], 1)
            totals = bank[6][:, 0:NE].unsqueeze(2).to_broadcast([128, NE, CPE])
            then(dve.tensor_tensor(full[:], totals, limits[:], ALU.is_gt))
            then(dve.tensor_reduce(e_tiles[:], full[:], AX.X, ALU.add))
            src, n = e_tiles, 0
            for step in (1, 2, 4, 8, 16):
                dst = sums[n % 2]
                dve.tensor_copy(dst[:, 0:step], src[:, 0:step])
                then(dve.tensor_tensor(dst[:, step:NE], src[:, step:NE], src[:, 0:NE - step], ALU.add))
                src, n = dst, n + 1
            dve.tensor_scalar(group_used[:], group_first[:], src[0:1, NE - 1:NE], None, ALU.is_lt)
            then(dve.tensor_scalar(passed[:], src[:], tile_no[:], None, ALU.is_le))
            dve.tensor_reduce(group_count[:], group_used[:], AX.X, ALU.add)
            dve.tensor_tensor(passed_tiles[:], passed[:], e_tiles[:], ALU.mult)
            then(dve.tensor_reduce(tile_expert[:], passed[:], AX.X, ALU.add))
            then(dve.tensor_reduce(tile_first[:], passed_tiles[:], AX.X, ALU.add))
            then(dve.scalar_tensor_tensor(tile_chunk[:], tile_expert[:], float(CPE), tile_no[:], ALU.mult, ALU.add))
            dve.tensor_tensor(chunk_idx[:], tile_chunk[:], tile_first[:], ALU.subtract
                              ).then_inc(S["chunk_ready"], 1)
            dve.tensor_copy(groups_run[:], group_count[:]).then_inc(S["groups_ready"], 1)
            dve.tensor_scalar(tile_expert[:], tile_expert[:], float(NE - 1), None, ALU.min
                              ).then_inc(S["tiles_listed"], 1)
            dve.wait_ge(S["expert_turned"], 1)
            dve.tensor_copy(expert_row[:], bank[5][0:1, 0:128]).then_inc(S["expert_ready"], 1)
            for w, dst in enumerate((slot_token, slot_gate)):
                dve.wait_ge(S["list_turned"], w + 1)
                dve.tensor_copy(dst[:], bank[w][0:SLOTS, 0:128]).then_inc(S["list_copied"], 1)

            def copy_x(i, p):
                dve.wait_ge(S["x_turned"], i + 1)
                if not (isinstance(i, int) and i < 2):
                    dve.wait_ge(S["up_done"], HC * (i - 1))
                dve.tensor_copy(x_T[p][:].rearrange("p g s -> p (g s)"), bank[6 + p][0:HALF, 0:2 * SLOTS]
                                ).then_inc(S["x_copied"], 1)

            def weigh(i, p, turns):
                dve.wait_ge(S["down_done"], i + 1)
                dve.wait_ge(b2_in[p], 16 * turns)
                if not (isinstance(i, int) and i < 2):
                    dve.wait_ge(S["y_out"], 16 * (i - 1))
                dve.tensor_tensor(y_rows[p][:], bank[4 + p][0:SLOTS, 0:D], b2_sb[p][:],
                                  ALU.add).then_inc(S["y_added"], 1)
                dve.wait_ge(S["y_added"], i + 1)
                dve.tensor_scalar(y_rows[p][:], y_rows[p][:], slot_gate[:, bass.ds(i, 1)], None,
                                  ALU.mult).then_inc(S["y_done"], 1)

            def two(q, first=False):
                for p in range(2):
                    i = 2 * q + p
                    copy_x(i + 1, (p + 1) % 2)
                    if not (first and p == 0):
                        weigh(i - 1, (p + 1) % 2, q + p)
            copy_x(0, 0)
            two(0, first=True)
            with dve.Fori(1, SURE // 2) as q:
                two(q)
            groups = groups_needed(dve)
            n = X_BUFS * groups + SURE
            with dve.Fori(SURE // 2, TILES // 2) as q:
                with dve.If(2 * q < n):
                    two(q)
            weigh(X_BUFS * groups + SURE - 1, 1, 2 * groups + SURE // 2)


def kernel(x, txt, L0_tok_W, L0_tok_bias, L0_attn_qkv_w, L0_attn_qkv_b, L0_attn_proj_w, L0_attn_proj_b,
           L0_ffn_Wg, L0_ffn_bg, L0_ffn_We, L0_ffn_be, L0_ffn_W1, L0_ffn_b1, L0_ffn_W2, L0_ffn_b2):
    import numpy as np
    import concourse.bacc as bacc
    from concourse.bass_utils import run_bass_kernel_spmd

    def weight(w, bias):
        w, bias = np.asarray(w), np.asarray(bias)
        rows = np.zeros((HALF + 1, 2, w.shape[1]), w.dtype)
        rows[0:HALF] = w.reshape(2, HALF, -1).transpose(1, 0, 2)
        rows[HALF, 1] = bias
        return rows

    img = np.asarray(x).reshape(B, 3, 6, 16, 6, 16)
    patches = img.transpose(0, 1, 3, 5, 2, 4).reshape(B, PK, 128, PATCH_TOK)
    grouped = np.zeros((GROUPS, 128, PK, GROUP, PATCH_TOK), patches.dtype)
    for b in range(B):
        grouped[b // GROUP, :, :, b % GROUP] = patches[b].transpose(1, 0, 2)
    router = np.concatenate([np.asarray(L0_ffn_Wg),
                             np.asarray(L0_ffn_We).transpose(1, 0, 2).reshape(D, NE)], axis=1)
    router_b = np.concatenate([np.asarray(L0_ffn_bg), np.asarray(L0_ffn_be).reshape(NE)])
    entries = np.zeros((T, B, KG * KE, 2), np.float32)
    entries[..., 0] = (np.arange(B) * T + np.arange(T)[:, None])[..., None]
    blank = np.zeros((128, CHUNKS // 128, SLOTS, 2), np.float32)
    blank[..., 0] = TOKENS + np.arange(SLOTS)
    arrays = {
        "patches": grouped.reshape(GROUPS, 128, PK, GROUP_ROWS),
        "tok_w": np.asarray(L0_tok_W).T.reshape(PK, 128, D).transpose(1, 0, 2),
        "tok_b": np.broadcast_to(np.asarray(L0_tok_bias), (GROUP_ROWS, D)),
        "txt": np.asarray(txt).transpose(1, 0, 2),
        "qkv_w": weight(np.asarray(L0_attn_qkv_w).T, L0_attn_qkv_b),
        "proj_w": weight(np.asarray(L0_attn_proj_w).T, L0_attn_proj_b),
        "router_w": weight(router, router_b),
        "w1": np.asarray(L0_ffn_W1).reshape(NE, 2, HALF, HID).transpose(0, 2, 1, 3),
        "b1": np.asarray(L0_ffn_b1).reshape(NE, HC, 128).transpose(0, 2, 1),
        "w2": np.asarray(L0_ffn_W2).reshape(NE, HC, 128, D).transpose(0, 2, 1, 3),
        "b2": np.asarray(L0_ffn_b2).reshape(NE, D),
        "identity": np.eye(T, dtype=np.float32),
        "head_mask": np.kron(np.eye(HG, dtype=np.float32), np.ones((HD, 1), np.float32)),
        "earlier": np.broadcast_to(np.tri(E, E, -1, dtype=np.float32), (T, E, E)),
        "later_c": np.tri(T, T, -1, dtype=np.float32).T,
        "region_c": np.broadcast_to(np.arange(NE, dtype=np.float32) * CPE * SLOTS, (T, NE)),
        "ranks8_c": np.broadcast_to(np.arange(E, dtype=np.float32), (T, E)),
        "entries_c": entries,
        "limits_c": np.broadcast_to(np.arange(CPE, dtype=np.float32) * SLOTS, (128, NE, CPE)),
        "tile_no_c": np.arange(128, dtype=np.float32)[:, None],
        "ident128_c": np.eye(128, dtype=np.float32),
        "group_first_c": (SURE + X_BUFS * np.arange(SPARE_GROUPS, dtype=np.float32))[None, :],
        "blank_c": blank,
    }
    arrays = {n: np.ascontiguousarray(a) for n, a in arrays.items()}
    nc = bacc.Bacc("TRN2", target_bir_lowering=False, num_devices=1)
    args = {n: nc.dram_tensor(f"in_{n}", a.shape, mybir.dt.from_np(a.dtype), kind="ExternalInput").ap()
            for n, a in arrays.items()}
    xf_rows = nc.dram_tensor("xf_rows", (TOKENS + SLOTS, D), F32, kind="Internal").ap()
    table = nc.dram_tensor("table", (CHUNKS * SLOTS, 2), F32, kind="Internal").ap()
    out = nc.dram_tensor("out", (TOKENS + SLOTS, D), F32, kind="ExternalOutput").ap()
    build(nc, xf_rows=xf_rows, table=table, out=out, **args)
    result = run_bass_kernel_spmd(nc, [{f"in_{n}": a for n, a in arrays.items()}], core_ids=[0])
    return np.ascontiguousarray(result.results[0]["out"][0:TOKENS].reshape(B, T, D))
```
